# Optimizing a Trainium2 kernel written in Bass

```python
import numpy as np
import jax
import jax.numpy as jnp

def _softmax(x, axis=-1):
    return jax.nn.softmax(x, axis=axis)

def _gelu(x):
    return jax.nn.gelu(x, approximate=True)

def _silu(x):
    return jax.nn.silu(x)

def _sigmoid(x):
    return jax.nn.sigmoid(x)

def _layernorm(x, axis=-1, eps=1e-05):
    m = jnp.mean(x, axis=axis, keepdims=True)
    v = jnp.var(x, axis=axis, keepdims=True)
    return (x - m) / jnp.sqrt(v + eps)

def _scatter_add(tgt, idx, src, axis=0):
    return tgt.at[idx].add(src)

def _segment_sum(src, seg, n):
    return jax.ops.segment_sum(src, seg, n)
kernel_name = 'mk_seq_preln_d1_jaxref_r8_15c86d'

def setup_inputs(seed: int=0):
    np.random.seed(seed)
    _w = jnp.asarray

    def _L0_attn_setup():
        import jax, jax.numpy as jnp
        import numpy as np
        DIM = 128
        DIM_INNER = 192
        BATCH = 4
        SEQ = 512

        def log_g(x):
            return jnp.where(x >= 0, jnp.log(jax.nn.relu(x) + 0.5), -jax.nn.softplus(-x))

        def associative_scan_log(log_coeffs, log_values):
            a_star = jnp.cumsum(log_coeffs, axis=1)
            log_h0_plus_b = jax.lax.cumlogsumexp(log_values - a_star, axis=1)
            return a_star + log_h0_plus_b

        def _reference_tuple_inner(x, W_hg, b_hg, W_out, b_out, h0):
            seq_len = x.shape[1]
            hg = jnp.einsum('bsd,ed->bse', x, W_hg) + b_hg
            hidden, gate = jnp.split(hg, 2, axis=-1)
            log_coeffs = -jax.nn.softplus(gate)
            log_z = -jax.nn.softplus(-gate)
            log_values = log_z + log_g(hidden)
            prev_log_hidden = jnp.broadcast_to(log_g(h0)[None, None, :], (x.shape[0], 1, h0.shape[0]))
            log_values = jnp.concatenate([prev_log_hidden, log_values], axis=1)
            log_coeffs = jnp.pad(log_coeffs, ((0, 0), (1, 0), (0, 0)))
            log_out = associative_scan_log(log_coeffs, log_values)
            out = jnp.exp(log_out[:, -seq_len:])
            next_hidden = out[:, -1:]
            next_log_hidden = log_out[:, -1:]
            y = jnp.einsum('bsd,ed->bse', out, W_out) + b_out
            return (y, next_hidden, next_log_hidden)
        key = jax.random.key(seed)
        ks = jax.random.split(key, 6)
        s_in = 1.0 / np.sqrt(DIM)
        s_out = 1.0 / np.sqrt(DIM_INNER)
        return {'x': jax.random.normal(ks[0], (BATCH, SEQ, DIM), jnp.float32), 'W_hg': jax.random.normal(ks[1], (2 * DIM_INNER, DIM), jnp.float32) * s_in, 'b_hg': jnp.zeros((2 * DIM_INNER,), jnp.float32), 'W_out': jax.random.normal(ks[2], (DIM, DIM_INNER), jnp.float32) * s_out, 'b_out': jnp.zeros((DIM,), jnp.float32), 'h0': jax.random.normal(ks[3], (DIM_INNER,), jnp.float32)}
    _L0_attn_in = _L0_attn_setup()

    def _L0_ffn_setup():
        import jax, jax.numpy as jnp
        import numpy as np
        B, S, D, H, E, F, K = (2, 128, 128, 16, 8, 512, 2)
        EPS = 1e-05

        def _layernorm(x, g, b):
            mu = jnp.mean(x, axis=-1, keepdims=True)
            var = jnp.mean(jnp.square(x - mu), axis=-1, keepdims=True)
            return (x - mu) * jax.lax.rsqrt(var + EPS) * g + b
        key = jax.random.key(seed)
        ks = jax.random.split(key, 12)
        w = lambda k, shape: jax.random.normal(k, shape, dtype=jnp.float32) * 0.02
        return {'x': jax.random.normal(ks[0], (B, S, D), dtype=jnp.float32), 'ln1_g': jnp.ones((D,), jnp.float32), 'ln1_b': jnp.zeros((D,), jnp.float32), 'ln2_g': jnp.ones((D,), jnp.float32), 'ln2_b': jnp.zeros((D,), jnp.float32), 'Wq': w(ks[1], (D, D)), 'Wk': w(ks[2], (D, D)), 'Wv': w(ks[3], (D, D)), 'Wo': w(ks[4], (D, D)), 'Wg': w(ks[5], (D, E)), 'W1': w(ks[6], (E, D, F)), 'b1': jnp.zeros((E, F), jnp.float32), 'W2': w(ks[7], (E, F, D)), 'b2': jnp.zeros((E, D), jnp.float32)}
    _L0_ffn_in = _L0_ffn_setup()
    _d = {'L0_attn_x': _L0_attn_in['x'], 'L0_attn_W_hg': _L0_attn_in['W_hg'], 'L0_attn_b_hg': _L0_attn_in['b_hg'], 'L0_attn_W_out': _L0_attn_in['W_out'], 'L0_attn_b_out': _L0_attn_in['b_out'], 'L0_attn_h0': _L0_attn_in['h0'], 'L0_ffn_ln1_g': _L0_ffn_in['ln1_g'], 'L0_ffn_ln1_b': _L0_ffn_in['ln1_b'], 'L0_ffn_ln2_g': _L0_ffn_in['ln2_g'], 'L0_ffn_ln2_b': _L0_ffn_in['ln2_b'], 'L0_ffn_Wq': _L0_ffn_in['Wq'], 'L0_ffn_Wk': _L0_ffn_in['Wk'], 'L0_ffn_Wv': _L0_ffn_in['Wv'], 'L0_ffn_Wo': _L0_ffn_in['Wo'], 'L0_ffn_Wg': _L0_ffn_in['Wg'], 'L0_ffn_W1': _L0_ffn_in['W1'], 'L0_ffn_b1': _L0_ffn_in['b1'], 'L0_ffn_W2': _L0_ffn_in['W2'], 'L0_ffn_b2': _L0_ffn_in['b2']}
    _x0 = _d['L0_attn_x']
    _d['L0_attn_x'] = jax.random.normal(jax.random.fold_in(jax.random.key(seed), 1), (32, 256, 128), dtype=_x0.dtype)
    del _x0
    return _d

def reference(L0_attn_x, L0_attn_W_hg, L0_attn_b_hg, L0_attn_W_out, L0_attn_b_out, L0_attn_h0, L0_ffn_ln1_g, L0_ffn_ln1_b, L0_ffn_ln2_g, L0_ffn_ln2_b, L0_ffn_Wq, L0_ffn_Wk, L0_ffn_Wv, L0_ffn_Wo, L0_ffn_Wg, L0_ffn_W1, L0_ffn_b1, L0_ffn_W2, L0_ffn_b2):

    def _L0_attn_ref(x, W_hg, b_hg, W_out, b_out, h0):
        import jax, jax.numpy as jnp
        import numpy as np
        DIM = 128
        DIM_INNER = 192
        BATCH = 4
        SEQ = 512

        def log_g(x):
            return jnp.where(x >= 0, jnp.log(jax.nn.relu(x) + 0.5), -jax.nn.softplus(-x))

        def associative_scan_log(log_coeffs, log_values):
            a_star = jnp.cumsum(log_coeffs, axis=1)
            log_h0_plus_b = jax.lax.cumlogsumexp(log_values - a_star, axis=1)
            return a_star + log_h0_plus_b

        def _reference_tuple_inner(x, W_hg, b_hg, W_out, b_out, h0):
            seq_len = x.shape[1]
            hg = jnp.einsum('bsd,ed->bse', x, W_hg) + b_hg
            hidden, gate = jnp.split(hg, 2, axis=-1)
            log_coeffs = -jax.nn.softplus(gate)
            log_z = -jax.nn.softplus(-gate)
            log_values = log_z + log_g(hidden)
            prev_log_hidden = jnp.broadcast_to(log_g(h0)[None, None, :], (x.shape[0], 1, h0.shape[0]))
            log_values = jnp.concatenate([prev_log_hidden, log_values], axis=1)
            log_coeffs = jnp.pad(log_coeffs, ((0, 0), (1, 0), (0, 0)))
            log_out = associative_scan_log(log_coeffs, log_values)
            out = jnp.exp(log_out[:, -seq_len:])
            next_hidden = out[:, -1:]
            next_log_hidden = log_out[:, -1:]
            y = jnp.einsum('bsd,ed->bse', out, W_out) + b_out
            return (y, next_hidden, next_log_hidden)
        return _reference_tuple_inner(x, W_hg, b_hg, W_out, b_out, h0)[0]

    def _L0_ffn_ref(x, ln1_g, ln1_b, ln2_g, ln2_b, Wq, Wk, Wv, Wo, Wg, W1, b1, W2, b2):
        import jax, jax.numpy as jnp
        import numpy as np
        B, S, D, H, E, F, K = (2, 128, 128, 16, 8, 512, 2)
        EPS = 1e-05

        def _layernorm(x, g, b):
            mu = jnp.mean(x, axis=-1, keepdims=True)
            var = jnp.mean(jnp.square(x - mu), axis=-1, keepdims=True)
            return (x - mu) * jax.lax.rsqrt(var + EPS) * g + b
        Bb, Ss, Dd = x.shape
        Dh = Dd // H
        h = _layernorm(x, ln1_g, ln1_b)
        q = (h @ Wq).reshape(Bb, Ss, H, Dh)
        k = (h @ Wk).reshape(Bb, Ss, H, Dh)
        v = (h @ Wv).reshape(Bb, Ss, H, Dh)
        scores = jnp.einsum('bqhd,bkhd->bhqk', q, k) / jnp.sqrt(jnp.float32(Dh))
        attn = jax.nn.softmax(scores, axis=-1)
        ctx = jnp.einsum('bhqk,bkhd->bqhd', attn, v).reshape(Bb, Ss, Dd)
        x = x + ctx @ Wo
        m = _layernorm(x, ln2_g, ln2_b)
        xt = m.reshape(-1, Dd)
        T = xt.shape[0]
        probs = jax.nn.softmax(xt @ Wg, axis=-1)
        wts, idx = jax.lax.top_k(probs, K)
        wts = wts / jnp.sum(wts, axis=-1, keepdims=True)
        h1 = jax.nn.gelu(jnp.einsum('td,edf->etf', xt, W1) + b1[:, None, :])
        ye = jnp.einsum('etf,efd->etd', h1, W2) + b2[:, None, :]
        sel = ye[idx, jnp.arange(T)[:, None], :]
        moe_out = jnp.sum(wts[..., None] * sel, axis=1).reshape(Bb, Ss, Dd)
        return x + moe_out
    x = L0_attn_x
    x = x + _L0_attn_ref(_layernorm(x, axis=-1), L0_attn_W_hg, L0_attn_b_hg, L0_attn_W_out, L0_attn_b_out, L0_attn_h0)
    x = x + _L0_ffn_ref(_layernorm(x, axis=-1), L0_ffn_ln1_g, L0_ffn_ln1_b, L0_ffn_ln2_g, L0_ffn_ln2_b, L0_ffn_Wq, L0_ffn_Wk, L0_ffn_Wv, L0_ffn_Wo, L0_ffn_Wg, L0_ffn_W1, L0_ffn_b1, L0_ffn_W2, L0_ffn_b2)
    return x

_drawn_inputs = setup_inputs


def setup_inputs(seed=0):
    import zlib

    import numpy as np

    out = dict(_drawn_inputs(seed))
    spreads = {'L0_attn_b_hg': (0.0, 0.1),
     'L0_attn_b_out': (0.0, 0.1),
     'L0_ffn_ln1_g': (1.0, 0.6),
     'L0_ffn_ln1_b': (0.0, 0.8),
     'L0_ffn_ln2_g': (1.0, 0.6),
     'L0_ffn_ln2_b': (0.0, 0.8),
     'L0_ffn_b1': (0.0, 0.8),
     'L0_ffn_b2': (0.0, 0.28)}
    factors = {'L0_attn_h0': 3.165,
     'L0_ffn_Wq': 8.0,
     'L0_ffn_Wk': 8.0,
     'L0_ffn_Wv': 3.4,
     'L0_ffn_Wo': 3.972,
     'L0_ffn_W1': 3.478,
     'L0_ffn_W2': 3.185}
    for name, (base, spread) in spreads.items():
        noise = np.random.default_rng([zlib.crc32(name.encode()), seed]).standard_normal(out[name].shape)
        drawn = base * np.exp(spread * noise) if base else spread * noise
        out[name] = jnp.asarray(drawn.astype(out[name].dtype))
    for name, factor in factors.items():
        out[name] = (out[name] * factor).astype(out[name].dtype)
    return out
```

```python
from contextlib import ExitStack

import numpy as np
import concourse.bass as bass
from concourse import mybir

ALU = mybir.AluOpType
ACT = mybir.ActivationFunctionType
AX = mybir.AxisListType
F32 = mybir.dt.float32
F16 = mybir.dt.float16
I32 = mybir.dt.int32
U32 = mybir.dt.uint32

P = 128
D = 128
NB, SL = 32, 256
T = NB * SL
NT = T // P
NG = NT // 4
DI = 192
HC = DI // 2
H, DH = 16, 8
NE, F = 8, 512
FC = F // P
BS = 256
NBLK = -(-(2 * T // BS + NE - 1) // 4) * 4
EPS = 1e-5
MUL = 32.0
BIG = 3.0e38

C_ID = 0
C_MASK = C_ID + P
C_TRI = C_MASK + 5
C_KEY = C_TRI + P
C_END = C_KEY + NE


def constants():
    c = np.zeros((P, C_END), np.float32)
    c[:, C_ID:C_ID + P] = np.eye(P)
    sel = np.zeros((P, 5, 4, P), np.float16)
    for g in range(4):
        for j in range(4):
            h = 4 * g + j
            for d in range(DH):
                sel[8 * h + d, 0, g, 32 * j + d] = 1
                sel[8 * h + d, 0, g, 32 * j + 8 + d] = 1
                sel[8 * h + d, 1, g, 32 * j + 16 + d] = 1
                sel[8 * h + d, 2, g, 32 * j + d] = 1
                sel[8 * h + d, 2, g, 32 * j + 16 + d] = 1
                sel[8 * h + d, 3, g, 32 * j + 8 + d] = 1
            sel[h, 4, g, 32 * j + 24] = 1
    for j in range(4):
        c[32 * j:32 * j + 32, C_MASK + j] = 1
        c[32 * j + 24, C_MASK + 4] = MUL
    c[:, C_TRI:C_TRI + P] = np.triu(np.ones((P, P)), 1)
    c[:, C_KEY:C_KEY + NE] = NE - np.arange(NE)
    blocks = np.arange(NBLK, dtype=np.float32)[None]
    return c, sel.reshape(P, -1), blocks


def layer_kernel(nc, x, w_hg, b_hg, w_out, b_out, h0, g1, be1, g2, be2, wq, wk, wv, wo, wg, w1, b1,
                 w2, b2, const, const_sel, const_blk, out):
    x_tok = x.rearrange("b (m p) d -> p (b m) d", p=P)
    out_tok = out.rearrange("b (m p) d -> p (b m) d", p=P)
    xs = nc.dram_tensor("expert_in", (NBLK * BS, D), F32, kind="Internal").ap()
    ys = nc.dram_tensor("expert_out", (NBLK * BS, D), F32, kind="Internal").ap()

    ctx = ExitStack()
    with ctx:
        def sb(name, shape, dt=F32):
            return ctx.enter_context(nc.sbuf_tensor(name, shape, dt))

        def sem(name):
            return ctx.enter_context(nc.semaphore(name))

        bank = [ctx.enter_context(nc.psum_tensor(f"bank{k}", [P, 512], F32)) for k in range(8)]

        cst = sb("cst", [P, C_END])
        ident = cst[:, C_ID:C_ID + P]
        mask = [cst[:, C_MASK + j:C_MASK + j + 1] for j in range(5)]
        sel = sb("sel", [P, 5, 4, P], F16)
        blkn = sb("blkn", [1, NBLK])
        ones = sb("ones", [P, P])
        X = sb("X", [P, NT, D])
        HT = sb("HT", [P, T])
        MH = HT[:, :].rearrange("p (n d) -> p n d", d=D)
        Z = sb("Z", [P, NT, D])
        zflat = Z[:, :, :].rearrange("p n d -> p (n d)")
        mom = sb("mom", [P, 4, 6])
        ssum, sdif, sm2, sq = (sb(n, [P, 4]) for n in ("ssum", "sdif", "sm2", "sq"))
        mean, var, vare, rstd, var2, r12 = ([sb(f"{n}{s}", [P, 4]) for s in range(2)] for n in
                                            ("mean", "var", "vare", "rstd", "var2", "r12"))
        epsc = sb("epsc", [P, 4])
        mhalf = sb("mhalf", [P, 4])
        xh = [sb(f"xh{s}", [P, 4, D]) for s in range(2)]
        whg = sb("whg", [P, 4, HC])
        bhg = sb("bhg", [HC, 4])
        nbg = sb("nbg", [HC, 2])
        wout = sb("wout", [HC + 1, 2, D])
        h0s = sb("h0s", [HC, 2])
        h0g = sb("h0g", [HC, 2])
        h0t = sb("h0t", [HC, 2])
        aff = sb("aff", [P, 4])
        wqk = sb("wqk", [P, 2, D])
        wvo = sb("wvo", [P, 2, D])
        wgs = sb("wgs", [P, NE])
        b1s = sb("b1s", [P, NE * FC])
        b2s = sb("b2s", [P, NE, D])
        wst = [sb(f"wst{s}", [P, F]) for s in range(2)]
        w1h, w1l, w2h, w2l = (sb(n, [P, NE, F], F16) for n in ("w1h", "w1l", "w2h", "w2l"))
        KM = [sb(f"KM{s}", [P, 4, 4, SL], F16) for s in range(2)]
        VA = [sb(f"VA{s}", [P, 2, H, 32]) for s in range(2)]
        arena = sb("arena", [P, 6912])
        at = [0]

        def view(n, dt=F32):
            words = n if dt == F32 else n // 2
            v = arena[:, at[0]:at[0] + words]
            at[0] += words
            assert at[0] <= 6912
            return v if dt == F32 else v.bitcast(dt)

        def gate_view(k, s):
            return zflat[0:HC, (2 * k + s) * 1024:(2 * k + s + 1) * 1024].rearrange("p (u t) -> p u t", u=2)
        zg, ag, sh, hv = ([gate_view(k, s) for s in range(2)] for k in range(4))
        ot = [view(1024)[0:HC + 1, :].rearrange("p (u t) -> p u t", u=2) for _ in range(2)]
        zero = view(512)
        at[0] = 0
        htb = [view(SL) for _ in range(2)]
        hi = view(512, F16)
        lo = view(512, F16)
        KA = view(1024, F16).rearrange("p (g t) -> p g t", g=4)
        QA = view(1024, F16).rearrange("p (g t) -> p g t", g=4)
        QM = [view(1024, F16).rearrange("p (g t) -> p g t", g=4) for _ in range(2)]
        nmax = view(2 * H).rearrange("p (t h) -> p t h", t=2)
        nmt = view(SL, F16)
        PT = [view(512) for _ in range(4)]
        CT = view(1024).rearrange("p (g t) -> p g t", g=4)
        rden = view(2 * H).rearrange("p (t h) -> p t h", t=2)
        CN = view(2 * D).rearrange("p (t d) -> p t d", t=2)
        CNT = view(SL)
        at[0] = 0
        MT = [view(512) for _ in range(2)]
        at[0] = 1024
        lg, key, oh1, oh2, l2, ohs, cum, dst, prd = (view(512) for _ in range(9))
        m1, m2, r1, r2, w_1, w_2, dif, d1f, d2f = (view(NT) for _ in range(9))
        tot, off, nblk, endb, cnti = (view(NE) for _ in range(5))
        blkc = view(NBLK * NE)[0:1, :].rearrange("p (b e) -> p b e", e=NE)
        blkf = sb("blkf", [1, NBLK])
        blke = sb("blke", [1, NBLK], I32)
        cntn = sb("cntn", [P, NE], I32)
        idx = sb("idx", [P, 2, NT], U32)
        wts = sb("wts", [P, 2, NT])
        at[0] = 0
        XB = [view(2 * D).rearrange("p (h d) -> p h d", h=2) for _ in range(4)]
        xm = view(BS)
        xmh = [view(BS, F16) for _ in range(2)]
        xml = [view(BS, F16) for _ in range(2)]
        G32 = [view(FC * BS) for _ in range(2)]
        GH = [view(FC * BS, F16) for _ in range(2)]
        GL = [view(FC * BS, F16) for _ in range(2)]
        YB = [view(2 * D).rearrange("p (h d) -> p h d", h=2) for _ in range(2)]
        at[0] = 0
        gat = [view(2 * D).rearrange("p (k d) -> p k d", k=2) for _ in range(8)]
        ob = [view(4 * D).rearrange("p (n d) -> p n d", n=4) for _ in range(2)]
        cmb = view(D)

        params_in = sem("params_in")
        bias_ready = sem("bias_ready")
        x_in = [sem(f"x_in{k}") for k in range(2)]
        dve_own = sem("dve_own")
        pool_own = sem("pool_own")
        zero_ready = sem("zero_ready")
        rows_clear = sem("rows_clear")
        ones_ready = sem("ones_ready")
        row_ones = sem("row_ones")
        preset = sem("preset")
        norm1 = sem("norm1")
        rs1 = sem("rs1")
        xh1 = sem("xh1")
        tp1 = sem("tp1")
        xt_ready = sem("xt_ready")
        hg_done = sem("hg_done")
        act_gates = sem("act_gates")
        relu_done = sem("relu_done")
        g_ready = sem("g_ready")
        v_ready = sem("v_ready")
        scan_done = sem("scan_done")
        y_done = sem("y_done")
        x1_ready = sem("x1_ready")
        norm3 = sem("norm3")
        rs3 = sem("rs3")
        xh3 = sem("xh3")
        z_ready = sem("z_ready")
        tp3 = sem("tp3")
        ht_ready = sem("ht_ready")
        htb_ready = sem("htb_ready")
        qk_done = sem("qk_done")
        v_done = sem("v_done")
        hi_ready = sem("hi_ready")
        lo_ready = sem("lo_ready")
        va_ready = sem("va_ready")
        selk_done = sem("selk_done")
        ka_ready = sem("ka_ready")
        km_ready = sem("km_ready")
        selq_done = sem("selq_done")
        qa_ready = sem("qa_ready")
        s_done = sem("s_done")
        max_done = sem("max_done")
        nmt_done = sem("nmt_done")
        nmt_ready = sem("nmt_ready")
        selm_done = sem("selm_done")
        qm_ready = sem("qm_ready")
        st_done = sem("st_done")
        exp_done = sem("exp_done")
        pv_done = sem("pv_done")
        ct_ready = sem("ct_ready")
        ctt_done = sem("ctt_done")
        cn_ready = sem("cn_ready")
        cnt_done = sem("cnt_done")
        cnt_ready = sem("cnt_ready")
        wo_done = sem("wo_done")
        x3_ready = sem("x3_ready")
        wst_in = [sem(f"wst_in{k}") for k in range(2)]
        wsplit = sem("wsplit")
        norm5 = sem("norm5")
        rs5 = sem("rs5")
        xh5 = sem("xh5")
        tp5 = sem("tp5")
        mt_ready = sem("mt_ready")
        mh_ready = sem("mh_ready")
        base_ready = sem("base_ready")
        lg_done = sem("lg_done")
        tot_ready = sem("tot_ready")
        cnt_sum = sem("cnt_sum")
        dif_ready = sem("dif_ready")
        exp6 = sem("exp6")
        idx_ready = sem("idx_ready")
        tab_ready = sem("tab_ready")
        scattered = sem("scattered")
        xb_in = [sem(f"xb_in{k}") for k in range(4)]
        tp7 = sem("tp7")
        xmh_ready = sem("xmh_ready")
        xml_ready = sem("xml_ready")
        up_done = sem("up_done")
        gelu_done = sem("gelu_done")
        gl_ready = sem("gl_ready")
        down_done = sem("down_done")
        yb_ready = sem("yb_ready")
        yb_out = [sem(f"yb_out{k}") for k in range(2)]
        gat_in = [sem(f"gat_in{k}") for k in range(8)]
        comb = sem("comb")
        o_out = [sem(f"o_out{k}") for k in range(2)]
        den_ready = sem("den_ready")
        xm_own = sem("xm_own")
        gh_own = sem("gh_own")
        cmb_own = sem("cmb_own")

        NPAR = 19

        def flat(ap):
            return ap.rearrange("p a d -> p (a d)")

        def tile(buf, n):
            return flat(buf[:, bass.ds(n, 1), :])

        def tiles(buf, i):
            return buf[:, bass.ds(4 * i, 4), :]

        def cols(buf, i, n):
            return buf[:, bass.ds(i * n, n)]

        def used(eng, sem_, n):
            if not isinstance(n, int) or n >= 1:
                eng.wait_ge(sem_, n)

        def two_by_two(eng, n, body):
            body(0, 0)
            body(1, 1)
            with eng.Fori(1, n // 2) as r:
                for s in range(2):
                    body(2 * r + s, s)

        def peeled(eng, n, body):
            body(1, 1)
            body(2, 0)
            with eng.Fori(1, (n - 2) // 2) as r:
                for s in range(2):
                    body(2 * r + 1 + s, 1 - s)

        def skewed(eng, n, first, second):
            first(0, 0)
            for i in range(2):
                first(i + 1, 1 - i)
                second(i, i)
            with eng.Fori(1, (n - 2) // 2) as r:
                for s in range(2):
                    first(2 * r + s + 1, 1 - s)
                    second(2 * r + s, s)
            first(n - 1, 1)
            second(n - 2, 0)
            second(n - 1, 1)

        def blocks(eng, first, body):
            for b in range(first, 4):
                body(b, b % 4)
            with eng.Fori(1, NBLK // 4 - 2) as r:
                for q in range(4):
                    body(4 * r + q, q)
            for b in range(NBLK - 8, NBLK):
                body(b, b % 4)

        def exists(b):
            return not isinstance(b, int) or 0 <= b < NBLK

        block = ctx.enter_context(nc.Block())

        @block.sync
        def _(sp):
            def par(dst, src):
                sp.dma_start(dst, src).then_inc(params_in, 16)

            def load_x(i, s):
                sp.dma_start(tiles(X, i), x_tok[:, bass.ds(4 * i, 4), :]).then_inc(x_in[s], 16)

            load_x(0, 0)
            load_x(1, 1)
            par(cst[:, :], const)
            par(sel[:, :, :, :].rearrange("p a g c -> p (a g c)"), const_sel)
            par(blkn[:, :], const_blk)
            par(whg[:, :, :], w_hg.rearrange("d (k c) -> d k c", c=HC))
            par(bhg[:, :], b_hg)
            par(wout[0:HC, :, :], w_out.rearrange("(u c) d -> c u d", c=HC))
            par(wout[HC:HC + 1, 1, :], b_out)
            par(h0s[:, :], h0)
            par(aff[:, 0:1], g1)
            par(aff[:, 1:2], be1)
            par(aff[:, 2:3], g2)
            par(aff[:, 3:4], be2)
            par(wqk[:, 0, :], wq)
            par(wqk[:, 1, :], wk)
            par(wvo[:, 0, :], wv)
            par(wvo[:, 1, :], wo)
            par(wgs[:, :], wg)
            par(b1s[:, :], b1)
            par(b2s[:, :, :], b2.rearrange("(a e) d -> a e d", a=1).broadcast_to([P, NE, D]))
            with sp.Fori(1, NG // 2) as r:
                for s in range(2):
                    sp.wait_ge(x_in[s], 16 * r)
                    load_x(2 * r + s, s)
            sp.wait_ge(zero_ready, 1)
            rows = NBLK * BS // P
            xz = xs.rearrange("(p r) d -> p (r d)", r=rows)
            for k in range(rows * D // 512):
                sp.dma_start(xz[:, 512 * k:512 * k + 512], zero).then_inc(rows_clear, 16)
            for k in range(2 * NE):
                if k >= 2:
                    sp.wait_ge(wsplit, 2 * (k - 1))
                e = k % NE
                if k < NE:
                    sp.dma_start(wst[k % 2][:, :], w1[e]).then_inc(wst_in[k % 2], 16)
                else:
                    sp.dma_start(wst[k % 2][:, :].rearrange("p (c f) -> p c f", c=FC),
                                 w2[e].rearrange("(c f) d -> f c d", f=P)).then_inc(wst_in[k % 2], 16)
            def store_block(b, s):
                sp.wait_ge(yb_ready, b + 1)
                sp.dma_start(ys[bass.ds(b * BS, BS), :].rearrange("(h p) d -> p h d", p=P), YB[s])\
                  .then_inc(yb_out[s], 16)

            blocks(sp, 0, lambda b, q: store_block(b, q % 2))
            for i in range(NG):
                sp.wait_ge(comb, 4 * i + 4)
                sp.dma_start(out_tok[:, 4 * i:4 * i + 4, :], ob[i % 2]).then_inc(o_out[i % 2], 16)
            for s in range(2):
                sp.wait_ge(o_out[s], 16 * NG // 2)

        @block.gpsimd
        def _(pool):
            nc.gpsimd.memset(zero, 0.0).then_inc(zero_ready, 1)
            nc.gpsimd.memset(mhalf[:, :], -0.5).then_inc(preset, 1)
            nc.gpsimd.memset(epsc[:, :], EPS).then_inc(preset, 1)
            nc.gpsimd.memset(ones[:, :], 1.0).then_inc(ones_ready, 1)
            for s in range(2):
                nc.gpsimd.memset(VA[s][:, :, :, :], 0.0).then_inc(pool_own, 1)
            pool.wait_ge(pool_own, 2)
            for s in range(2):
                nc.gpsimd.memset(VA[s][:, :, :, DH:DH + 1], 1.0).then_inc(preset, 1)
            pool.wait_ge(preset, 4)

            def rsqrt(i, s, ready, done):
                pool.wait_ge(ready, i + 1)
                nc.gpsimd.tensor_tensor(rstd[s][:, :], vare[s][:, :], mhalf[:, :], ALU.pow).then_inc(done, 1)

            two_by_two(pool, NG, lambda i, s: rsqrt(i, s, norm1, rs1))

            def values_step(i, s):
                for u in range(2):
                    pool.wait_ge(g_ready, 2 * i + u + 1)
                    nc.gpsimd.tensor_tensor(zg[s][:, u, :], zg[s][:, u, :], hv[s][:, u, :], ALU.mult)\
                        .then_inc(v_ready, 1)

            two_by_two(pool, NG, values_step)

            def rsqrt_twice(i, s):
                rsqrt(i, s, norm3, pool_own)
                k = 5 * i + 2
                pool.wait_ge(pool_own, k + 1)
                nc.gpsimd.tensor_tensor(var2[s][:, :], var[s][:, :], rstd[s][:, :], ALU.mult).then_inc(pool_own, 1)
                pool.wait_ge(pool_own, k + 2)
                nc.gpsimd.tensor_tensor(var2[s][:, :], var2[s][:, :], rstd[s][:, :], ALU.mult).then_inc(pool_own, 1)
                pool.wait_ge(pool_own, k + 3)
                nc.gpsimd.tensor_tensor(var2[s][:, :], var2[s][:, :], epsc[:, :], ALU.add).then_inc(pool_own, 1)
                pool.wait_ge(pool_own, k + 4)
                nc.gpsimd.tensor_tensor(r12[s][:, :], var2[s][:, :], mhalf[:, :], ALU.pow).then_inc(pool_own, 1)
                pool.wait_ge(pool_own, k + 5)
                nc.gpsimd.tensor_tensor(r12[s][:, :], r12[s][:, :], rstd[s][:, :], ALU.mult).then_inc(rs3, 1)

            two_by_two(pool, NG, rsqrt_twice)

            def slice_step(b, s):
                nc.gpsimd.tensor_copy(htb[s], cols(HT, b, SL)).then_inc(htb_ready, 1)

            pool.wait_ge(ht_ready, 1)
            pool.wait_ge(rows_clear, 16 * (NBLK * BS // 512))
            slice_step(0, 0)
            slice_step(1, 1)
            for k in range(2 * NE):
                whi, wlo = (w1h, w1l) if k < NE else (w2h, w2l)
                e, src = k % NE, wst[k % 2][:, :]
                pool.wait_ge(wst_in[k % 2], 16 * (k // 2 + 1))
                nc.gpsimd.tensor_copy(whi[:, e, :], src).then_inc(wsplit, 1)
                pool.wait_ge(wsplit, 2 * k + 1)
                nc.gpsimd.tensor_tensor(wlo[:, e, :], src, whi[:, e, :], ALU.subtract).then_inc(wsplit, 1)
            pool.wait_ge(ht_ready, NG)

            def next_slice(b, s):
                pool.wait_ge(v_done, b - 1)
                slice_step(b, s)

            with pool.Fori(1, NB // 2) as r:
                for s in range(2):
                    next_slice(2 * r + s, s)

            def norm5_step(i, s):
                rsqrt(i, s, norm5, rs5)
                nc.gpsimd.tensor_tensor(tiles(X, i), tiles(X, i), tiles(Z, i), ALU.add).then_inc(base_ready, 1)

            two_by_two(pool, NG, norm5_step)

            pool.wait_ge(rows_clear, 16 * (NBLK * BS // 512))
            pool.wait_ge(mh_ready, NG)
            pool.wait_ge(idx_ready, 1)
            for n in range(NT):
                for k in range(2):
                    pool.indirect_dma_start(xs, bass.IndirectOffsetOnAxis(idx[:, k, n:n + 1], 0),
                                            MH[:, n, :], None).then_inc(scattered, 16)
            pool.wait_ge(yb_out[0], 16 * NBLK // 2)
            pool.wait_ge(yb_out[1], 16 * NBLK // 2)
            for n in range(NT):
                if n >= 8:
                    pool.wait_ge(comb, n - 7)
                for k in range(2):
                    pool.indirect_dma_start(gat[n % 8][:, k, :], None, ys,
                                            bass.IndirectOffsetOnAxis(idx[:, k, n:n + 1], 0))\
                        .then_inc(gat_in[n % 8], 16)

        @block.scalar
        def _(act):
            def copy(dst, src):
                return nc.scalar.activation(dst, src, ACT.Copy)

            def evac1(i, s):
                act.wait_ge(tp1, i + 1)
                copy(cols(HT, i, 512), bank[6 + s][:, :]).then_inc(xt_ready, 1)

            two_by_two(act, NG, evac1)
            act.wait_ge(bias_ready, 1)
            nc.scalar.activation(h0g[:, :], h0s[:, :], ACT.Sigmoid).then_inc(act_gates, 1)

            def gates(i, s):
                used(act, scan_done, 4 * (i - 1))
                for u in range(2):
                    act.wait_ge(hg_done, 2 * i + u + 1)
                    H_, G_ = bank[2 * u][0:HC, :], bank[2 * u + 1][0:HC, :]
                    nc.scalar.activation(zg[s][:, u, :], G_, ACT.Sigmoid, bias=bhg[:, 2 + u:3 + u])
                    nc.scalar.activation(ag[s][:, u, :], G_, ACT.Sigmoid, bias=nbg[:, u:u + 1], scale=-1.0)
                    nc.scalar.activation(sh[s][:, u, :], H_, ACT.Sigmoid, bias=bhg[:, u:u + 1])\
                        .then_inc(act_gates, 1)

            gates(0, 0)
            peeled(act, NG, gates)
            gates(NG - 1, 1)

            def evac3(i, s):
                act.wait_ge(tp3, i + 1)
                nc.scalar.activation(cols(HT, i, 512), bank[6 + s][:, :], ACT.Identity,
                                     bias=aff[:, 1:2], scale=aff[:, 0:1]).then_inc(ht_ready, 1)

            two_by_two(act, NG, evac3)

            def front_hi(n):
                act.wait_ge(qk_done, n + 1)
                copy(hi, bank[6][:, :]).then_inc(hi_ready, 1)

            def front_ka(n):
                used(act, km_ready, n)
                for half in range(2):
                    act.wait_ge(selk_done, 2 * n + half + 1)
                    nc.scalar.activation(flat(KA[:, 2 * half:2 * half + 2, :]), bank[6 + half][:, :],
                                         ACT.Identity, bias=mask[4]).then_inc(ka_ready, 1)

            def front_qa(n):
                for half in range(2):
                    act.wait_ge(selq_done, 2 * n + half + 1)
                    copy(flat(QA[:, 2 * half:2 * half + 2, :]), bank[6 + half][:, :]).then_inc(qa_ready, 1)

            def front_qm(n, s):
                for half in range(2):
                    act.wait_ge(selm_done, 2 * n + half + 1)
                    copy(flat(QM[s][:, 2 * half:2 * half + 2, :]), bank[7 - half][:, :]).then_inc(qm_ready, 1)

            def exp_step(b, c):
                act.wait_ge(st_done, 16 * b + c + 1)
                used(act, pv_done, 16 * b + c - 3)
                nc.scalar.activation(PT[c % 4], bank[2 + c % 2][:, :], ACT.Exp, scale=DH ** -0.5)\
                    .then_inc(exp_done, 1)

            def ctx_evac(b, pair):
                act.wait_ge(pv_done, 16 * b + 8 * pair + 8)
                used(act, ctt_done, 2 * b)
                copy(flat(CT[:, 2 * pair:2 * pair + 2, :]), bank[4 + pair][:, :]).then_inc(ct_ready, 1)

            def attention(b, s, front=True):
                if front:
                    front_hi(b + 1)
                exp_step(b, 0)
                exp_step(b, 1)
                if front:
                    front_ka(b + 1)
                exp_step(b, 2)
                if front:
                    front_qa(b + 1)
                for c in range(3, 16):
                    exp_step(b, c)
                    if c == 11:
                        ctx_evac(b, 0)
                if front:
                    front_qm(b + 1, 1 - s)
                ctx_evac(b, 1)

            front_hi(0)
            front_ka(0)
            front_qa(0)
            front_qm(0, 0)
            attention(0, 0)
            peeled(act, NB, attention)
            attention(NB - 1, 1, front=False)

            def evac5(i, s):
                act.wait_ge(tp5, i + 1)
                used(act, lg_done, i - 1)
                nc.scalar.activation(MT[s], bank[6 + s][:, :], ACT.Identity,
                                     bias=aff[:, 3:4], scale=aff[:, 2:3]).then_inc(mt_ready, 1)

            two_by_two(act, NG, evac5)
            act.wait_ge(dif_ready, 1)
            nc.scalar.activation(w_2, dif, ACT.Exp).then_inc(exp6, 1)

            act.wait_ge(tab_ready, 1)

            def load_block(b, q):
                act.dma_start(XB[q], xs[bass.ds(b * BS, BS), :].rearrange("(h p) d -> p h d", p=P))\
                  .then_inc(xb_in[q], 16)

            def x_hi(b, q):
                s = q % 2
                act.wait_ge(tp7, b + 1)
                if exists(b + 4):
                    load_block(b + 4, q)
                used(act, up_done, b - 1)
                nc.scalar.activation(xmh[s], bank[s][:, 0:BS], ACT.Identity,
                                     bias=aff[:, 3:4], scale=aff[:, 2:3]).then_inc(xmh_ready, 1)

            def gelu(b, s):
                e = act.value_load(blke[0:1, bass.ds(b, 1)], min_val=0, max_val=NE - 1)
                act.wait_ge(up_done, b + 1)
                used(act, gl_ready, b - 1)
                for c in range(FC):
                    last = nc.scalar.activation(G32[s][:, BS * c:BS * c + BS],
                                                bank[2 + 2 * s + c // 2][:, BS * (c % 2):BS * (c % 2) + BS],
                                                ACT.Gelu_apprx_tanh, bias=b1s[:, bass.ds(e * FC + c, 1)])
                last.then_inc(gelu_done, 1)

            def experts(b, q):
                if exists(b + 3):
                    x_hi(b + 3, (q + 3) % 4)
                if exists(b + 2):
                    gelu(b + 2, q % 2)

            act.wait_ge(scattered, 16 * 2 * NT)
            for q in range(4):
                load_block(q, q)
            blocks(act, -3, experts)

        @block.vector
        def _(dve):
            V = nc.vector
            count = [0]

            for s in range(2):
                V.memset(ot[s][HC:HC + 1, :, :], 1.0).then_inc(row_ones, 1)
            dve.wait_ge(params_in, 16 * NPAR)
            V.tensor_scalar(nbg[:, :], bhg[:, 2:4], -1.0, None, ALU.mult)
            V.tensor_scalar(h0t[:, :], h0s[:, :], 0.0, None, ALU.max).then_inc(bias_ready, 1)
            for s in range(2):
                V.memset(KM[s][:, :, :, :].rearrange("p g j t -> p (g j t)").bitcast(F32), 0.0)

            def moments(i, s, buf, base, done):
                k = base + 3 * i
                for t in range(4):
                    last = V.bn_stats(mom[:, t, :], tile(buf, 4 * i + t))
                last.then_inc(dve_own, 1)
                dve.wait_ge(dve_own, k + 1)
                V.tensor_tensor(ssum[:, :], mom[:, :, 1], mom[:, :, 4], ALU.add)
                V.tensor_tensor(sdif[:, :], mom[:, :, 1], mom[:, :, 4], ALU.subtract)
                V.tensor_tensor(sm2[:, :], mom[:, :, 2], mom[:, :, 5], ALU.add).then_inc(dve_own, 1)
                dve.wait_ge(dve_own, k + 2)
                V.tensor_scalar(mean[s][:, :], ssum[:, :], 0.5, None, ALU.mult)
                V.scalar_tensor_tensor(sq[:, :], sdif[:, :], 0.25, sdif[:, :], ALU.mult, ALU.mult)
                V.tensor_scalar(sm2[:, :], sm2[:, :], 1.0 / D, None, ALU.mult).then_inc(dve_own, 1)
                dve.wait_ge(dve_own, k + 3)
                V.tensor_tensor(var[s][:, :], sm2[:, :], sq[:, :], ALU.add)
                V.scalar_tensor_tensor(vare[s][:, :], sm2[:, :], EPS, sq[:, :], ALU.add, ALU.add).then_inc(done, 1)

            def normed(i, s, buf, rs, done, dst=None, src=None):
                for t in range(4):
                    last = V.tensor_scalar(xh[s][:, t, :] if dst is None else tile(dst, 4 * i + t),
                                           tile(buf, 4 * i + t), mean[s][:, t:t + 1],
                                           (src or rstd)[s][:, t:t + 1], ALU.subtract, ALU.mult)
                if done is not None:
                    last.then_inc(done, 1)

            def moments1(i, s):
                dve.wait_ge(x_in[s], 8 * (i - s) + 16)
                moments(i, s, X, 0, norm1)

            def normed1(i, s):
                dve.wait_ge(rs1, i + 1)
                used(dve, tp1, i - 1)
                normed(i, s, X, rs1, xh1)

            skewed(dve, NG, moments1, normed1)
            own1 = 3 * NG
            dve.wait_ge(act_gates, 1)
            V.scalar_tensor_tensor(h0g[:, :], h0g[:, :], 0.5, h0t[:, :], ALU.min, ALU.add).then_inc(dve_own, 1)
            dve.wait_ge(dve_own, own1 + 1)

            def gates(i, s):
                for u in range(2):
                    dve.wait_ge(act_gates, 2 * i + u + 2)
                    V.tensor_scalar(hv[s][:, u, :], bank[2 * u][0:HC, :], bhg[:, u:u + 1], 0.0,
                                    ALU.add, ALU.max).then_inc(relu_done, 1)
                    dve.wait_ge(relu_done, 2 * i + u + 1)
                    V.scalar_tensor_tensor(hv[s][:, u, :], sh[s][:, u, :], 0.5, hv[s][:, u, :],
                                           ALU.min, ALU.add).then_inc(g_ready, 1)

            def scans(i, s):
                for u in range(2):
                    dve.wait_ge(v_ready, 2 * i + u + 1)
                    for b in range(2):
                        t = slice(SL * b, SL * b + SL)
                        V.tensor_tensor_scan(ot[s][0:HC, u, t], ag[s][:, u, t], zg[s][:, u, t],
                                             h0g[:, u:u + 1], ALU.mult, ALU.add).then_inc(scan_done, 1)

            def add_y(i, s):
                dve.wait_ge(y_done, i + 1)
                V.tensor_tensor(tiles(X, i), bank[4 + s][:, :].rearrange("p (n d) -> p n d", d=D),
                                tiles(X, i), ALU.add).then_inc(x1_ready, 1)

            def recurrence(i, s):
                gates(i, s)
                add_y(i - 1, 1 - s)
                scans(i, s)

            gates(0, 0)
            scans(0, 0)
            peeled(dve, NG, recurrence)
            recurrence(NG - 1, 1)
            add_y(NG - 1, 1)

            def moments3(i, s):
                dve.wait_ge(x1_ready, i + 1)
                moments(i, s, X, own1 + 1, norm3)

            def normed3(i, s):
                dve.wait_ge(rs3, i + 1)
                used(dve, tp3, i - 1)
                normed(i, s, X, rs3, xh3, src=r12)
                normed(i, s, X, rs3, z_ready, dst=Z)

            skewed(dve, NG, moments3, normed3)
            own3 = own1 + 1 + 3 * NG

            def front_split(n, s):
                dve.wait_ge(hi_ready, n + 1)
                V.scalar_tensor_tensor(lo, hi, -1.0, bank[6][:, :], ALU.mult, ALU.add).then_inc(lo_ready, 1)
                dve.wait_ge(v_done, n + 1)
                used(dve, pv_done, 16 * (n - 1))
                V.tensor_copy(VA[s][:, :, :, 0:DH],
                              bank[7][:, 0:2 * D].rearrange("p (k h d) -> p k h d", k=2, d=DH))\
                    .then_inc(va_ready, 1)

            def front_mask(n, s):
                dve.wait_ge(ka_ready, 2 * n + 2)
                used(dve, st_done, 16 * (n - 1))
                for j in range(4):
                    last = V.tensor_scalar(KM[s][:, :, j, :], KA, mask[j], None, ALU.mult)
                last.then_inc(km_ready, 1)

            def front_max(n):
                for c in range(16):
                    g, qt, jp = c // 4, c // 2 % 2, c % 2
                    dve.wait_ge(s_done, 16 * n + c + 1)
                    V.tensor_reduce(nmax[:, qt, 4 * g + 2 * jp:4 * g + 2 * jp + 2],
                                    bank[c % 2][:, :].rearrange("p (j t) -> p j t", j=2),
                                    AX.X, ALU.max, negate=True).then_inc(max_done, 1)
                dve.wait_ge(nmt_done, n + 1)
                V.tensor_scalar(nmt[0:H, :], bank[6][0:H, 0:SL], 1.0 / MUL, None, ALU.mult)\
                    .then_inc(nmt_ready, 1)

            def tail_norm(m):
                for qt in range(2):
                    dve.wait_ge(ctt_done, 2 * m + qt + 1)
                    src = bank[6 + qt][:, :].rearrange("p (h r) -> p h r", r=32)
                    V.reciprocal(rden[:, qt, :], src[:, :, DH]).then_inc(den_ready, 1)
                    dve.wait_ge(den_ready, 2 * m + qt + 1)
                    V.tensor_tensor(CN[:, qt, :].rearrange("p (h d) -> p h d", d=DH), src[:, :, 0:DH],
                                    rden[:, qt, :, None].broadcast_to([P, H, DH]), ALU.mult)\
                        .then_inc(cn_ready, 1)

            def tail_out(m):
                dve.wait_ge(cnt_done, m + 1)
                V.tensor_copy(CNT, bank[6][:, 0:SL]).then_inc(cnt_ready, 1)
                dve.wait_ge(wo_done, m + 1)
                z2 = Z[:, bass.ds(2 * m, 2), :]
                V.tensor_tensor(z2, bank[7][:, 0:2 * D].rearrange("p (n d) -> p n d", d=D), z2, ALU.add)\
                    .then_inc(x3_ready, 1)

            def attention(b, s, front=True, tail=True):
                if front:
                    front_split(b + 1, 1 - s)
                if tail:
                    tail_norm(b - 1)
                if front:
                    front_mask(b + 1, 1 - s)
                if tail:
                    tail_out(b - 1)
                if front:
                    front_max(b + 1)

            dve.wait_ge(preset, 4)
            dve.wait_ge(ht_ready, NG)
            V.memset(nmt, 0.0)
            front_split(0, 0)
            front_mask(0, 0)
            front_max(0)
            attention(0, 0, tail=False)
            peeled(dve, NB, attention)
            attention(NB - 1, 1, front=False)
            tail_norm(NB - 1)
            tail_out(NB - 1)

            def moments5(i, s):
                dve.wait_ge(x3_ready, 2 * i + 2)
                moments(i, s, Z, own3, norm5)

            def normed5(i, s):
                dve.wait_ge(rs5, i + 1)
                used(dve, tp5, i - 1)
                normed(i, s, Z, rs5, xh5)
                normed(i, s, Z, rs5, mh_ready, dst=MH)

            skewed(dve, NG, moments5, normed5)

            k = [own3 + 3 * NG]

            def step(ins):
                ins.then_inc(dve_own, 1)
                k[0] += 1
                dve.wait_ge(dve_own, k[0])

            def by_tile(v):
                return v.rearrange("p (n e) -> p n e", e=NE)

            def by_expert(v):
                return v.rearrange("p (e n) -> p e n", e=NE)

            def over_e(v):
                return v[:, :, None].broadcast_to([P, NT, NE])

            keys = cst[:, None, C_KEY:C_KEY + NE].broadcast_to([P, NT, NE])
            dve.wait_ge(lg_done, NG)
            dve.wait_ge(ones_ready, 1)
            step(V.tensor_copy(lg, bank[0][:, :]))
            for src, oh, m, r in ((lg, oh1, m1, r1), (l2, oh2, m2, r2)):
                step(V.tensor_reduce(m, by_tile(src), AX.X, ALU.max))
                step(V.tensor_tensor(by_tile(key), by_tile(src), over_e(m), ALU.is_equal))
                step(V.tensor_tensor(by_tile(key), by_tile(key), keys, ALU.mult))
                step(V.tensor_reduce(r, by_tile(key), AX.X, ALU.max))
                step(V.tensor_tensor(by_tile(oh), by_tile(key), over_e(r), ALU.is_equal))
                if src is lg:
                    step(V.scalar_tensor_tensor(l2, oh1, -BIG, lg, ALU.mult, ALU.add))
            V.tensor_tensor(dif, m2, m1, ALU.subtract).then_inc(dif_ready, 1)
            step(V.tensor_tensor(by_expert(ohs).rearrange("p e n -> p n e"), by_tile(oh1), by_tile(oh2), ALU.add))
            V.tensor_reduce(tot, by_expert(ohs), AX.X, ALU.add).then_inc(tot_ready, 1)
            step(V.tensor_tensor_scan(cum, ones[:, 0:1].broadcast_to([P, 512]), ohs, 0.0, ALU.mult, ALU.add))
            step(V.tensor_tensor(cum, cum, ohs, ALU.subtract))
            dve.wait_ge(cnt_sum, 1)
            step(V.tensor_scalar(cntn[:, :], bank[1][:, 0:NE], float(BS - 1), None, ALU.add))
            step(V.tensor_scalar(cntn[:, :], cntn[:, :], BS.bit_length() - 1, None, ALU.logical_shift_right))
            step(V.tensor_copy(nblk, cntn[:, :]))
            step(V.tensor_tensor_scan(endb, ones[:, 0:NE], nblk, 0.0, ALU.mult, ALU.add))
            step(V.tensor_tensor(off, endb, nblk, ALU.subtract))
            step(V.scalar_tensor_tensor(off, off, float(BS), bank[2][:, 0:NE], ALU.mult, ALU.add))
            step(V.tensor_tensor(off, off, by_expert(cum)[:, :, 0], ALU.subtract))
            step(V.tensor_tensor(by_expert(dst), by_expert(cum), off[:, :, None].broadcast_to([P, NE, NT]), ALU.add))
            for q, (oh, df) in enumerate(((oh1, d1f), (oh2, d2f))):
                step(V.tensor_tensor(by_tile(prd), by_tile(oh), by_expert(dst).rearrange("p e n -> p n e"), ALU.mult))
                step(V.tensor_reduce(df, by_tile(prd), AX.X, ALU.add))
                last = V.tensor_copy(idx[:, q, :], df)
            last.then_inc(idx_ready, 1)
            step(V.tensor_tensor(blkc, blkn[:, :, None].broadcast_to([1, NBLK, NE]),
                                 endb[0:1, None, :].broadcast_to([1, NBLK, NE]), ALU.is_ge))
            step(V.tensor_reduce(blkf[:, :], blkc, AX.X, ALU.add))
            V.tensor_scalar(blke[:, :], blkf[:, :], float(NE - 1), None, ALU.min).then_inc(tab_ready, 1)
            dve.wait_ge(exp6, 1)
            step(V.tensor_scalar(w_1, w_2, 1.0, None, ALU.add))
            step(V.reciprocal(wts[:, 0, :], w_1))
            step(V.tensor_tensor(wts[:, 1, :], w_2, wts[:, 0, :], ALU.mult))

            dve.wait_ge(tab_ready, 1)

            def x_lo(b, s):
                dve.wait_ge(xmh_ready, b + 1)
                used(dve, xml_ready, b)
                V.tensor_scalar(xm, bank[s][:, 0:BS], aff[:, 2:3], aff[:, 3:4], ALU.mult, ALU.add)\
                    .then_inc(xm_own, 1)
                dve.wait_ge(xm_own, b + 1)
                V.tensor_tensor(xml[s], xm, xmh[s], ALU.subtract).then_inc(xml_ready, 1)

            def split(b, s):
                dve.wait_ge(gelu_done, b + 1)
                used(dve, down_done, b - 1)
                V.tensor_copy(GH[s], G32[s]).then_inc(gh_own, 1)
                dve.wait_ge(gh_own, b + 1)
                V.tensor_tensor(GL[s], G32[s], GH[s], ALU.subtract).then_inc(gl_ready, 1)

            def y_out(b, s):
                e = dve.value_load(blke[0:1, bass.ds(b, 1)], min_val=0, max_val=NE - 1)
                dve.wait_ge(down_done, b + 1)
                used(dve, yb_out[s], 8 * (b - s))
                V.tensor_tensor(YB[s], bank[6 + s][:, 0:2 * D].rearrange("p (h d) -> p h d", d=D),
                                b2s[:, bass.ds(e, 1), :].broadcast_to([P, 2, D]), ALU.add).then_inc(yb_ready, 1)

            def experts(b, q):
                if exists(b + 3):
                    x_lo(b + 3, (q + 1) % 2)
                if exists(b + 1):
                    split(b + 1, (q + 1) % 2)
                if exists(b - 1):
                    y_out(b - 1, (q + 1) % 2)

            blocks(dve, -3, experts)
            y_out(NBLK - 1, 1)

            dve.wait_ge(base_ready, NG)
            dve.wait_ge(dve_own, k[0])
            for n in range(NT):
                i = n // 4
                dve.wait_ge(gat_in[n % 8], 32 * (n // 8 + 1))
                dve.wait_ge(comb, n)
                V.scalar_tensor_tensor(cmb, gat[n % 8][:, 0, :], wts[:, 0, n:n + 1], X[:, n, :],
                                       ALU.mult, ALU.add).then_inc(cmb_own, 1)
                if n % 4 == 0 and i >= 2:
                    dve.wait_ge(o_out[i % 2], 16 * (i // 2))
                dve.wait_ge(cmb_own, n + 1)
                V.scalar_tensor_tensor(ob[i % 2][:, n % 4, :], gat[n % 8][:, 1, :], wts[:, 1, n:n + 1], cmb,
                                       ALU.mult, ALU.add).then_inc(comb, 1)

        @block.tensor
        def _(pe):
            def mm(dst, lhsT, rhs, start=True, stop=True):
                return nc.tensor.matmul(dst, lhsT, rhs, start=start, stop=stop)

            def transposes(bk, src, done):
                for t in range(4):
                    last = nc.tensor.transpose(bk[:, P * t:P * t + P], src[:, t, :], ident)
                last.then_inc(done, 1)

            pe.wait_ge(params_in, 16 * NPAR)

            def tp1_step(i, s):
                pe.wait_ge(xh1, i + 1)
                used(pe, xt_ready, i - 1)
                transposes(bank[6 + s], xh[s], tp1)

            two_by_two(pe, NG, tp1_step)

            pe.wait_ge(row_ones, 2)

            def hidden_gate(i, s):
                pe.wait_ge(xt_ready, i + 1)
                for u in range(2):
                    used(pe, act_gates, 2 * i + u)
                    used(pe, relu_done, 2 * i + u - 1)
                    mm(bank[2 * u][0:HC, :], whg[:, u, :], cols(HT, i, 512))
                    mm(bank[2 * u + 1][0:HC, :], whg[:, 2 + u, :], cols(HT, i, 512)).then_inc(hg_done, 1)

            def y_step(i, s):
                pe.wait_ge(scan_done, 4 * i + 4)
                used(pe, x1_ready, i - 1)
                for t in range(4):
                    for u in range(2):
                        k = HC + u
                        last = mm(bank[4 + s][:, P * t:P * t + P], ot[s][0:k, u, P * t:P * t + P],
                                  wout[0:k, u, :], start=u == 0, stop=u == 1)
                last.then_inc(y_done, 1)

            skewed(pe, NG, hidden_gate, y_step)

            def tp3_step(i, s):
                pe.wait_ge(xh3, i + 1)
                used(pe, ht_ready, i - 1)
                transposes(bank[6 + s], xh[s], tp3)

            two_by_two(pe, NG, tp3_step)

            def proj(n, s):
                pe.wait_ge(htb_ready, n + 1)
                if isinstance(n, int) and n == 0:
                    pe.wait_ge(ht_ready, NG)
                else:
                    pe.wait_ge(qm_ready, 2 * n)
                mm(bank[6][:, 0:SL], wqk[:, 0, :], htb[s])
                mm(bank[6][:, SL:2 * SL], wqk[:, 1, :], htb[s]).then_inc(qk_done, 1)
                for kt in range(2):
                    last = mm(bank[7][:, P * kt:P * kt + P], htb[s][:, P * kt:P * kt + P], wvo[:, 0, :])
                last.then_inc(v_done, 1)

            def rows(n, parts, bk, half, done):
                for gi in range(2):
                    g = 2 * half + gi
                    for k, (sl, src) in enumerate(parts):
                        last = mm(bk[:, SL * gi:SL * gi + SL], sel[:, sl, g, :], src,
                                  start=k == 0, stop=k == len(parts) - 1)
                last.then_inc(done, 1)

            q_, k_ = slice(0, SL), slice(SL, 2 * SL)

            def sel_k(n, tail):
                pe.wait_ge(lo_ready, n + 1)
                pe.wait_ge(va_ready, n + 1)
                if tail:
                    pe.wait_ge(cn_ready, 2 * n - 2)
                for half in range(2):
                    rows(n, ((0, hi[:, k_]), (1, lo[:, k_])), bank[6 + half], half, selk_done)

            def sel_q(n):
                for half in range(2):
                    pe.wait_ge(ka_ready, 2 * n + half + 1)
                    rows(n, ((2, hi[:, q_]), (3, lo[:, q_])), bank[6 + half], half, selq_done)

            def s_chunk(n, s, c):
                g, qt, jp = c // 4, c // 2 % 2, c % 2
                if c == 0:
                    pe.wait_ge(km_ready, n + 1)
                if c % 8 == 0:
                    pe.wait_ge(qa_ready, 2 * n + c // 8 + 1)
                used(pe, max_done, 16 * n + c - 1)
                mm(bank[c % 2][:, :], QA[:, g, P * qt:P * qt + P],
                   KM[s][:, g, 2 * jp:2 * jp + 2, :]).then_inc(s_done, 1)

            def max_rows(n, tail):
                pe.wait_ge(max_done, 16 * n + 16)
                if tail:
                    pe.wait_ge(cnt_ready, n - 1)
                for qt in range(2):
                    last = mm(bank[6][0:H, P * qt:P * qt + P], nmax[:, qt, :], ident)
                last.then_inc(nmt_done, 1)

            def sel_m(n, tail):
                pe.wait_ge(nmt_ready, n + 1)
                if tail:
                    pe.wait_ge(x3_ready, n - 1)
                else:
                    pe.wait_ge(qa_ready, 2 * n + 2)
                for half in range(2):
                    rows(n, ((2, hi[:, q_]), (3, lo[:, q_]), (4, nmt)), bank[7 - half], half, selm_done)

            def st_chunk(b, s, c):
                g, kt, jp = c // 4, c // 2 % 2, c % 2
                if c % 8 == 0:
                    pe.wait_ge(qm_ready, 2 * b + c // 8 + 1)
                used(pe, exp_done, 16 * b + c - 1)
                for jj in range(2):
                    last = mm(bank[2 + c % 2][:, SL * jj:SL * jj + SL],
                              KM[s][:, g, 2 * jp + jj, P * kt:P * kt + P], QM[s][:, g, :])
                last.then_inc(st_done, 1)

            def pv(b, s, c):
                g, kt, jp = c // 4, c // 2 % 2, c % 2
                pe.wait_ge(exp_done, 16 * b + c + 1)
                if c == 0:
                    pe.wait_ge(va_ready, b + 1)
                if c % 8 == 0:
                    used(pe, ct_ready, 2 * b - 1 + c // 8)
                for jj in range(2):
                    j = 2 * jp + jj
                    last = mm(bank[4 + g // 2][32 * j:32 * j + 32, SL * (g % 2):SL * (g % 2) + SL],
                              VA[s][:, kt, 4 * g + j, :], PT[c % 4][:, SL * jj:SL * jj + SL],
                              start=kt == 0, stop=kt == 1)
                last.then_inc(pv_done, 1)

            def ctx_t(m, front):
                pe.wait_ge(ct_ready, 2 * m + 2)
                if front:
                    pe.wait_ge(lo_ready, m + 3)
                    pe.wait_ge(va_ready, m + 3)
                elif m == NB - 1:
                    pe.wait_ge(x3_ready, m)
                else:
                    pe.wait_ge(qm_ready, 2 * m + 4)
                for qt in range(2):
                    for g in range(4):
                        last = nc.tensor.transpose(bank[6 + qt][:, P * g:P * g + P],
                                                   CT[:, g, P * qt:P * qt + P], ident)
                    last.then_inc(ctt_done, 1)

            def ctx_n(m, front):
                pe.wait_ge(cn_ready, 2 * m + 2)
                if front:
                    pe.wait_ge(qa_ready, 2 * m + 5)
                for qt in range(2):
                    last = nc.tensor.transpose(bank[6][:, P * qt:P * qt + P], CN[:, qt, :], ident)
                last.then_inc(cnt_done, 1)

            def ctx_o(m, front):
                pe.wait_ge(cnt_ready, m + 1)
                if front:
                    pe.wait_ge(qa_ready, 2 * m + 6)
                for qt in range(2):
                    last = mm(bank[7][:, P * qt:P * qt + P], CNT[:, P * qt:P * qt + P], wvo[:, 1, :])
                last.then_inc(wo_done, 1)

            def attention(b, s, front=True, tail=True):
                n, ns = b + 1, 1 - s
                if front:
                    proj(n, ns)
                st_chunk(b, s, 0)
                st_chunk(b, s, 1)
                if tail:
                    ctx_t(b - 1, front)
                st_chunk(b, s, 2)
                pv(b, s, 0)
                if front:
                    sel_k(n, tail)
                st_chunk(b, s, 3)
                pv(b, s, 1)
                if front:
                    sel_q(n)
                if tail:
                    ctx_n(b - 1, front)
                st_chunk(b, s, 4)
                pv(b, s, 2)
                if tail:
                    ctx_o(b - 1, front)
                for c in range(5, 16):
                    st_chunk(b, s, c)
                    pv(b, s, c - 2)
                    if front and c < 13:
                        s_chunk(n, ns, 2 * (c - 5))
                        s_chunk(n, ns, 2 * (c - 5) + 1)
                if front:
                    max_rows(n, tail)
                pv(b, s, 14)
                if front:
                    sel_m(n, tail)
                pv(b, s, 15)

            proj(0, 0)
            sel_k(0, False)
            sel_q(0)
            for c in range(16):
                s_chunk(0, 0, c)
            max_rows(0, False)
            sel_m(0, False)
            attention(0, 0, tail=False)
            peeled(pe, NB, attention)
            attention(NB - 1, 1, front=False)
            ctx_t(NB - 1, False)
            ctx_n(NB - 1, False)
            ctx_o(NB - 1, False)

            def tp5_step(i, s):
                pe.wait_ge(xh5, i + 1)
                used(pe, mt_ready, i - 1)
                transposes(bank[6 + s], xh[s], tp5)

            def logits(i, s):
                pe.wait_ge(mt_ready, i + 1)
                for t in range(4):
                    last = mm(cols(bank[0], 4 * i + t, NE), MT[s][:, P * t:P * t + P], wgs[:, :])
                last.then_inc(lg_done, 1)

            pe.wait_ge(x3_ready, NB)
            skewed(pe, NG, tp5_step, logits)

            pe.wait_ge(tot_ready, 1)
            mm(bank[1][:, 0:NE], ones[:, 0:P], tot)
            mm(bank[2][:, 0:NE], cst[:, C_TRI:C_TRI + P], tot).then_inc(cnt_sum, 1)

            pe.wait_ge(tab_ready, 1)
            pe.wait_ge(wsplit, 4 * NE)

            def block_t(b, q):
                pe.wait_ge(xb_in[q], 4 * (b - q) + 16)
                used(pe, xml_ready, b - 1)
                for h in range(2):
                    last = nc.tensor.transpose(bank[q % 2][:, P * h:P * h + P], XB[q][:, h, :], ident)
                last.then_inc(tp7, 1)

            def expert_of(b):
                return pe.value_load(blke[0:1, bass.ds(b, 1)], min_val=0, max_val=NE - 1)

            def part(w, e, c):
                return w[:, bass.ds(e, 1), P * c:P * c + P].rearrange("p a f -> p (a f)")

            def up(b, s):
                e = expert_of(b)
                pe.wait_ge(xml_ready, b + 1)
                used(pe, gelu_done, b - 1)
                for c in range(FC):
                    dst = bank[2 + 2 * s + c // 2][:, BS * (c % 2):BS * (c % 2) + BS]
                    mm(dst, part(w1h, e, c), xmh[s], stop=False)
                    mm(dst, part(w1h, e, c), xml[s], start=False, stop=False)
                    last = mm(dst, part(w1l, e, c), xmh[s], start=False)
                last.then_inc(up_done, 1)

            def down(b, s):
                e = expert_of(b)
                pe.wait_ge(gl_ready, b + 1)
                used(pe, yb_ready, b - 1)
                for h in range(2):
                    dst = bank[6 + s][:, P * h:P * h + P]
                    for c in range(FC):
                        x = slice(BS * c + P * h, BS * c + P * h + P)
                        mm(dst, GH[s][:, x], part(w2h, e, c), start=c == 0, stop=False)
                        mm(dst, GH[s][:, x], part(w2l, e, c), start=False, stop=False)
                        last = mm(dst, GL[s][:, x], part(w2h, e, c), start=False, stop=c == FC - 1)
                last.then_inc(down_done, 1)

            def experts(b, q):
                if exists(b + 3):
                    block_t(b + 3, (q + 3) % 4)
                if exists(b + 2):
                    up(b + 2, q % 2)
                if exists(b):
                    down(b, q % 2)

            blocks(pe, -3, experts)


def kernel(**inputs):
    import concourse.bacc as bacc
    from concourse.bass_utils import run_bass_kernel_spmd

    a = {k: np.asarray(v) for k, v in inputs.items()}
    const, const_sel, const_blk = constants()
    arrays = {
        "x": a["L0_attn_x"],
        "w_hg": a["L0_attn_W_hg"].T,
        "b_hg": a["L0_attn_b_hg"].reshape(4, HC).T,
        "w_out": a["L0_attn_W_out"].T,
        "b_out": a["L0_attn_b_out"].reshape(1, D),
        "h0": a["L0_attn_h0"].reshape(2, HC).T,
        "g1": a["L0_ffn_ln1_g"].reshape(D, 1),
        "be1": a["L0_ffn_ln1_b"].reshape(D, 1),
        "g2": a["L0_ffn_ln2_g"].reshape(D, 1),
        "be2": a["L0_ffn_ln2_b"].reshape(D, 1),
        "wq": a["L0_ffn_Wq"],
        "wk": a["L0_ffn_Wk"],
        "wv": a["L0_ffn_Wv"],
        "wo": a["L0_ffn_Wo"],
        "wg": a["L0_ffn_Wg"],
        "w1": a["L0_ffn_W1"],
        "b1": a["L0_ffn_b1"].reshape(NE, FC, P).transpose(2, 0, 1).reshape(P, NE * FC),
        "w2": a["L0_ffn_W2"],
        "b2": a["L0_ffn_b2"],
        "const": const,
        "const_sel": const_sel,
        "const_blk": const_blk,
    }
    arrays = {k: np.ascontiguousarray(v) for k, v in arrays.items()}
    nc = bacc.Bacc("TRN2", target_bir_lowering=False, num_devices=1)
    args = [nc.dram_tensor(k, v.shape, mybir.dt.from_np(v.dtype), kind="ExternalInput").ap()
            for k, v in arrays.items()]
    args.append(nc.dram_tensor("out", (NB, SL, D), F32, kind="ExternalOutput").ap())
    layer_kernel(nc, *args)
    return run_bass_kernel_spmd(nc, [arrays], core_ids=[0]).results[0]["out"]
```

```python
from contextlib import ExitStack

import numpy as np
import concourse.bass as bass
from concourse import mybir

ALU = mybir.AluOpType
ACT = mybir.ActivationFunctionType
AX = mybir.AxisListType
F32 = mybir.dt.float32
F16 = mybir.dt.float16
I32 = mybir.dt.int32
U32 = mybir.dt.uint32

P = 128
D = 128
NB, SL = 32, 256
T = NB * SL
NT = T // P
NG = NT // 4
DI = 192
HC = DI // 2
H, DH = 16, 8
NE, F = 8, 512
FC = F // P
BS = 256
SEQ0 = [0, 3 * NB // 4, NB]
TILE0 = [q * SL // P for q in SEQ0]
GRP0 = [q // 2 for q in SEQ0]
BLK0 = [0]
for q0, q1 in zip(SEQ0, SEQ0[1:]):
    BLK0.append(BLK0[-1] + -(-(2 * (q1 - q0) * SL // BS + NE - 1) // 4) * 4)
NBLK = BLK0[-1]
HN, HBLK = TILE0[1], BLK0[1]
EPS = 1e-5
MUL = 32.0
BIG = 3.0e38

C_ID = 0
C_MASK = C_ID + P
C_TRI = C_MASK + 5
C_KEY = C_TRI + P
C_END = C_KEY + NE


def constants():
    c = np.zeros((P, C_END), np.float32)
    c[:, C_ID:C_ID + P] = np.eye(P)
    sel = np.zeros((P, 5, 4, P), np.float16)
    for g in range(4):
        for j in range(4):
            h = 4 * g + j
            for d in range(DH):
                sel[8 * h + d, 0, g, 32 * j + d] = 1
                sel[8 * h + d, 0, g, 32 * j + 8 + d] = 1
                sel[8 * h + d, 1, g, 32 * j + 16 + d] = 1
                sel[8 * h + d, 2, g, 32 * j + d] = 1
                sel[8 * h + d, 2, g, 32 * j + 16 + d] = 1
                sel[8 * h + d, 3, g, 32 * j + 8 + d] = 1
            sel[h, 4, g, 32 * j + 24] = 1
    for j in range(4):
        c[32 * j:32 * j + 32, C_MASK + j] = 1
        c[32 * j + 24, C_MASK + 4] = MUL
    c[:, C_TRI:C_TRI + P] = np.triu(np.ones((P, P)), 1)
    c[:, C_KEY:C_KEY + NE] = NE - np.arange(NE)
    blocks = np.arange(NBLK, dtype=np.float32)[None]
    return c, sel.reshape(P, -1), blocks


def layer_kernel(nc, x, w_hg, b_hg, w_out, b_out, h0, g1, be1, g2, be2, wq, wk, wv, wo, wg, w1, b1,
                 w2, b2, const, const_sel, const_blk, out):
    x_tok = x.rearrange("b (m p) d -> p (b m) d", p=P)
    out_tok = out.rearrange("b (m p) d -> p (b m) d", p=P)
    xs = nc.dram_tensor("expert_in", (NBLK * BS, D), F32, kind="Internal").ap()
    ys = nc.dram_tensor("expert_out", (NBLK * BS, D), F32, kind="Internal").ap()

    ctx = ExitStack()
    with ctx:
        def sb(name, shape, dt=F32):
            return ctx.enter_context(nc.sbuf_tensor(name, shape, dt))

        def sem(name):
            return ctx.enter_context(nc.semaphore(name))

        bank = [ctx.enter_context(nc.psum_tensor(f"bank{k}", [P, 512], F32)) for k in range(8)]

        cst = sb("cst", [P, C_END])
        ident = cst[:, C_ID:C_ID + P]
        mask = [cst[:, C_MASK + j:C_MASK + j + 1] for j in range(5)]
        sel = sb("sel", [P, 5, 4, P], F16)
        blkn = sb("blkn", [1, NBLK])
        ones = sb("ones", [P, P])
        X = sb("X", [P, NT, D])
        HT = sb("HT", [P, T])
        MH = HT[:, :].rearrange("p (n d) -> p n d", d=D)
        Z = sb("Z", [P, NT, D])
        zflat = Z[:, :, :].rearrange("p n d -> p (n d)")
        mom = sb("mom", [P, 4, 6])
        ssum, sdif, sm2, sq = (sb(n, [P, 4]) for n in ("ssum", "sdif", "sm2", "sq"))
        mean, var, vare, rstd, var2, r12 = ([sb(f"{n}{s}", [P, 4]) for s in range(2)] for n in
                                            ("mean", "var", "vare", "rstd", "var2", "r12"))
        nmr = [sb(f"nmr{s}", [P, 4]) for s in range(2)]
        epsc = sb("epsc", [P, 4])
        mhalf = sb("mhalf", [P, 4])
        xh = [sb(f"xh{s}", [P, 4, D]) for s in range(2)]
        whg = sb("whg", [P, 4, HC])
        bhg = sb("bhg", [HC, 4])
        nbg = sb("nbg", [HC, 2])
        wout = sb("wout", [HC + 1, 2, D])
        h0s = sb("h0s", [HC, 2])
        h0g = sb("h0g", [HC, 2])
        h0t = sb("h0t", [HC, 2])
        aff = sb("aff", [P, 4])
        wqk = sb("wqk", [P, 2, D])
        wvo = sb("wvo", [P, 2, D])
        wgs = sb("wgs", [P, NE])
        b1s = sb("b1s", [P, NE * FC])
        b2s = sb("b2s", [P, NE, D])
        wst = [sb(f"wst{s}", [P, F]) for s in range(2)]
        w1h, w1l, w2h, w2l = (sb(n, [P, NE, F], F16) for n in ("w1h", "w1l", "w2h", "w2l"))
        KM = [sb(f"KM{s}", [P, 4, 4, SL], F16) for s in range(2)]
        VA = [sb(f"VA{s}", [P, 2, H, 32]) for s in range(2)]
        arena = sb("arena", [P, 6976])
        at = [0]

        def view(n, dt=F32):
            words = n if dt == F32 else n // 2
            v = arena[:, at[0]:at[0] + words]
            at[0] += words
            assert at[0] <= 6976
            return v if dt == F32 else v.bitcast(dt)

        def flat4(buf):
            return buf[:, :, :].rearrange("p a d -> p (a d)")

        def gate_view(k, s):
            return zflat[0:HC, (2 * k + s) * 1024:(2 * k + s + 1) * 1024].rearrange("p (u t) -> p u t", u=2)
        zg, ag, sh, hv = ([gate_view(k, s) for s in range(2)] for k in range(4))
        ot = [view(1024)[0:HC + 1, :].rearrange("p (u t) -> p u t", u=2) for _ in range(2)]
        zero = view(512)
        at[0] = 0
        htb = [view(SL) for _ in range(2)]
        two = flat4(xh[1]).bitcast(F16)
        hi = [view(512, F16), two[:, 0:512]]
        lo = [view(512, F16), two[:, 512:1024]]
        KA = view(1024, F16).rearrange("p (g t) -> p g t", g=4)
        QA = [v.rearrange("p (g t) -> p g t", g=4) for v in (view(1024, F16), flat4(xh[0]).bitcast(F16))]
        QM = [view(1024, F16).rearrange("p (g t) -> p g t", g=4) for _ in range(2)]
        nmax = view(2 * H).rearrange("p (t h) -> p t h", t=2)
        nmt = [view(SL, F16) for _ in range(2)]
        PT = [view(512) for _ in range(4)]
        CT = view(1024).rearrange("p (g t) -> p g t", g=4)
        rden = view(2 * H).rearrange("p (t h) -> p t h", t=2)
        CN = view(2 * D).rearrange("p (t d) -> p t d", t=2)
        CNT = view(SL)
        at[0] = 0
        MT = [view(512) for _ in range(2)]
        at[0] = 1024
        by_pair = [view(HN * NE) for _ in range(9)]
        by_token = [view(HN) for _ in range(9)]
        w_2, dif = by_token[5:7]
        tot, off, nblk, endb, cnti = (view(NE) for _ in range(5))
        blkc = view(HBLK * NE)[0:1, :].rearrange("p (b e) -> p b e", e=NE)
        blkf = sb("blkf", [1, HBLK])
        blke = sb("blke", [1, NBLK], I32)
        cntn = sb("cntn", [P, NE], I32)
        idx = sb("idx", [P, 2, NT], U32)
        wts = sb("wts", [P, 2, NT])
        at[0] = 0
        XB = [view(2 * D).rearrange("p (h d) -> p h d", h=2) for _ in range(4)]
        xm = view(BS)
        xmh = [view(BS, F16) for _ in range(2)]
        xml = [view(BS, F16) for _ in range(2)]
        G32 = [view(FC * BS) for _ in range(2)]
        GH = [view(FC * BS, F16) for _ in range(2)]
        GL = [view(FC * BS, F16) for _ in range(2)]
        YB = [view(2 * D).rearrange("p (h d) -> p h d", h=2) for _ in range(2)]
        at[0] = 0
        gat = [Z, MH]
        ob = [view(4 * D).rearrange("p (n d) -> p n d", n=4) for _ in range(2)]
        cmb = view(4 * D).rearrange("p (n d) -> p n d", n=4)

        const_in = sem("const_in")
        params_in = sem("params_in")
        bias_ready = sem("bias_ready")
        x_in = [sem(f"x_in{k}") for k in range(2)]
        dve_own = sem("dve_own")
        pool_own = sem("pool_own")
        zero_ready = sem("zero_ready")
        rows_clear = sem("rows_clear")
        ones_ready = sem("ones_ready")
        row_ones = sem("row_ones")
        preset = sem("preset")
        norm1 = sem("norm1")
        rs1 = sem("rs1")
        xh1 = sem("xh1")
        tp1 = sem("tp1")
        xt_ready = sem("xt_ready")
        hg_done = sem("hg_done")
        act_gates = sem("act_gates")
        relu_done = sem("relu_done")
        g_ready = sem("g_ready")
        v_ready = sem("v_ready")
        scan_done = sem("scan_done")
        y_done = sem("y_done")
        x1_ready = sem("x1_ready")
        norm3 = sem("norm3")
        rs3 = sem("rs3")
        xh3 = sem("xh3")
        nmr_ready = sem("nmr_ready")
        z_ready = sem("z_ready")
        tp3 = sem("tp3")
        ht_ready = sem("ht_ready")
        htb_ready = sem("htb_ready")
        qk_done = sem("qk_done")
        v_done = sem("v_done")
        hi_ready = sem("hi_ready")
        lo_ready = sem("lo_ready")
        va_ready = sem("va_ready")
        selk_done = sem("selk_done")
        ka_ready = sem("ka_ready")
        km_ready = sem("km_ready")
        selq_done = sem("selq_done")
        qa_ready = sem("qa_ready")
        s_done = sem("s_done")
        max_done = sem("max_done")
        nmt_done = sem("nmt_done")
        nmt_ready = sem("nmt_ready")
        selm_done = sem("selm_done")
        qm_ready = sem("qm_ready")
        st_done = sem("st_done")
        exp_done = sem("exp_done")
        pv_done = sem("pv_done")
        ct_ready = sem("ct_ready")
        ctt_done = sem("ctt_done")
        cn_ready = sem("cn_ready")
        cnt_done = sem("cnt_done")
        cnt_ready = sem("cnt_ready")
        wo_done = sem("wo_done")
        x3_ready = sem("x3_ready")
        wst_in = [sem(f"wst_in{k}") for k in range(2)]
        wsplit = sem("wsplit")
        norm5 = sem("norm5")
        rs5 = sem("rs5")
        xh5 = sem("xh5")
        tp5 = sem("tp5")
        mt_ready = sem("mt_ready")
        mh_ready = sem("mh_ready")
        base_ready = sem("base_ready")
        lg_done = sem("lg_done")
        tot_ready = sem("tot_ready")
        cnt_sum = sem("cnt_sum")
        dif_ready = sem("dif_ready")
        exp6 = sem("exp6")
        idx_ready = sem("idx_ready")
        tab_ready = sem("tab_ready")
        route_done = sem("route_done")
        scattered = [sem(f"scattered{k}") for k in range(2)]
        xb_in = [sem(f"xb_in{k}") for k in range(4)]
        tp7 = sem("tp7")
        xmh_ready = sem("xmh_ready")
        xml_ready = sem("xml_ready")
        up_done = sem("up_done")
        gelu_done = sem("gelu_done")
        gl_ready = sem("gl_ready")
        down_done = sem("down_done")
        yb_ready = sem("yb_ready")
        yb_out = [sem(f"yb_out{k}") for k in range(2)]
        gat_in = [sem(f"gat_in{k}") for k in range(1 + GRP0[2] - GRP0[1])]
        comb = sem("comb")
        o_out = [sem(f"o_out{k}") for k in range(2)]
        den_ready = sem("den_ready")
        xm_own = sem("xm_own")
        gh_own = sem("gh_own")
        cmb_own = sem("cmb_own")

        NPAR = 18

        def flat(ap):
            return ap.rearrange("p a d -> p (a d)")

        def tile(buf, n):
            return flat(buf[:, bass.ds(n, 1), :])

        def tiles(buf, i):
            return buf[:, bass.ds(4 * i, 4), :]

        def cols(buf, i, n):
            return buf[:, bass.ds(i * n, n)]

        def used(eng, sem_, n):
            if not isinstance(n, int) or n >= 1:
                eng.wait_ge(sem_, n)

        def two_by_two(eng, n, body, lo=0):
            for i in range(2 * (lo == 0)):
                body(i, i)
            with eng.Fori(max(lo // 2, 1), n // 2) as r:
                for s in range(2):
                    body(2 * r + s, s)

        def peeled(eng, n, body):
            body(1, 1)
            body(2, 0)
            with eng.Fori(1, (n - 2) // 2) as r:
                for s in range(2):
                    body(2 * r + 1 + s, 1 - s)

        def sequences(eng, first, body):
            last = SEQ0[1 if first == 0 else 2] - 1
            body(first, 0, tail=False)
            body(first + 1, 1)
            with eng.Fori(first // 2 + 1, last // 2) as r:
                for s in range(2):
                    body(2 * r + s, s)
            body(last - 1, 0, front=False)
            body(last, 1, front=False, nxt=False)

        def skewed(eng, n, first, second, lo=0):
            first(lo, 0)
            for i in range(2 * (lo == 0)):
                first(i + 1, 1 - i)
                second(i, i)
            with eng.Fori(max(lo // 2, 1), (n - 2) // 2) as r:
                for s in range(2):
                    first(2 * r + s + 1, 1 - s)
                    second(2 * r + s, s)
            first(n - 1, 1)
            second(n - 2, 0)
            second(n - 1, 1)

        def blocks(eng, first, body, second_part=None):
            for b in range(first, 4):
                body(b, b % 4)
            cut = HBLK // 4 - 2
            for r0, r1 in ((1, cut), (cut, NBLK // 4 - 2)) if second_part else ((1, NBLK // 4 - 2),):
                if second_part and r0 == cut:
                    second_part()
                with eng.Fori(r0, r1) as r:
                    for q in range(4):
                        body(4 * r + q, q)
            for b in range(NBLK - 8, NBLK):
                body(b, b % 4)

        def exists(b):
            return not isinstance(b, int) or 0 <= b < NBLK

        block = ctx.enter_context(nc.Block())

        @block.sync
        def _(sp):
            def par(dst, src):
                sp.dma_start(dst, src).then_inc(params_in, 16)

            def load_x(i, s):
                sp.dma_start(tiles(X, i), x_tok[:, bass.ds(4 * i, 4), :]).then_inc(x_in[s], 16)

            load_x(0, 0)
            sp.dma_start(cst[:, :], const).then_inc(const_in, 16)
            load_x(1, 1)
            par(sel[:, :, :, :].rearrange("p a g c -> p (a g c)"), const_sel)
            par(blkn[:, :], const_blk)
            par(whg[:, :, :], w_hg.rearrange("d (k c) -> d k c", c=HC))
            par(bhg[:, :], b_hg)
            par(wout[0:HC, :, :], w_out.rearrange("(u c) d -> c u d", c=HC))
            par(wout[HC:HC + 1, 1, :], b_out)
            par(h0s[:, :], h0)
            par(aff[:, 0:1], g1)
            par(aff[:, 1:2], be1)
            par(aff[:, 2:3], g2)
            par(aff[:, 3:4], be2)
            par(wqk[:, 0, :], wq)
            par(wqk[:, 1, :], wk)
            par(wvo[:, 0, :], wv)
            par(wvo[:, 1, :], wo)
            par(wgs[:, :], wg)
            par(b1s[:, :], b1)
            par(b2s[:, :, :], b2.rearrange("(a e) d -> a e d", a=1).broadcast_to([P, NE, D]))
            with sp.Fori(1, NG // 2) as r:
                for s in range(2):
                    sp.wait_ge(x_in[s], 16 * r)
                    load_x(2 * r + s, s)
            sp.wait_ge(zero_ready, 1)
            rows = NBLK * BS // P
            xz = xs.rearrange("(p r) d -> p (r d)", r=rows)
            for k in range(rows * D // 512):
                sp.dma_start(xz[:, 512 * k:512 * k + 512], zero).then_inc(rows_clear, 16)
            for k in range(2 * NE):
                if k >= 2:
                    sp.wait_ge(wsplit, 2 * (k - 1))
                e = k % NE
                if k < NE:
                    sp.dma_start(wst[k % 2][:, :], w1[e]).then_inc(wst_in[k % 2], 16)
                else:
                    sp.dma_start(wst[k % 2][:, :].rearrange("p (c f) -> p c f", c=FC),
                                 w2[e].rearrange("(c f) d -> f c d", f=P)).then_inc(wst_in[k % 2], 16)
            def store_block(b, s):
                sp.wait_ge(yb_ready, b + 1)
                sp.dma_start(ys[bass.ds(b * BS, BS), :].rearrange("(h p) d -> p h d", p=P), YB[s])\
                  .then_inc(yb_out[s], 16)

            blocks(sp, 0, lambda b, q: store_block(b, q % 2))
            for i in range(NG):
                sp.wait_ge(comb, i + 1)
                sp.dma_start(out_tok[:, 4 * i:4 * i + 4, :], ob[i % 2]).then_inc(o_out[i % 2], 16)
            for s in range(2):
                sp.wait_ge(o_out[s], 16 * NG // 2)

        @block.gpsimd
        def _(pool):
            nc.gpsimd.memset(zero, 0.0).then_inc(zero_ready, 1)
            nc.gpsimd.memset(mhalf[:, :], -0.5).then_inc(preset, 1)
            nc.gpsimd.memset(epsc[:, :], EPS).then_inc(preset, 1)
            nc.gpsimd.memset(ones[:, :], 1.0).then_inc(ones_ready, 1)
            for s in range(2):
                nc.gpsimd.memset(VA[s][:, :, :, :], 0.0).then_inc(pool_own, 1)
            pool.wait_ge(pool_own, 2)
            for s in range(2):
                nc.gpsimd.memset(VA[s][:, :, :, DH:DH + 1], 1.0).then_inc(preset, 1)
            pool.wait_ge(preset, 4)

            def rsqrt(i, s, ready, done):
                pool.wait_ge(ready, i + 1)
                nc.gpsimd.tensor_tensor(rstd[s][:, :], vare[s][:, :], mhalf[:, :], ALU.pow).then_inc(done, 1)

            two_by_two(pool, NG, lambda i, s: rsqrt(i, s, norm1, rs1))

            def values_step(i, s):
                for u in range(2):
                    pool.wait_ge(g_ready, 2 * i + u + 1)
                    nc.gpsimd.tensor_tensor(zg[s][:, u, :], zg[s][:, u, :], hv[s][:, u, :], ALU.mult)\
                        .then_inc(v_ready, 1)

            two_by_two(pool, NG, values_step)

            def rsqrt_twice(i, s):
                used(pool, z_ready, i - 1)
                rsqrt(i, s, norm3, pool_own)
                k = 5 * i + 2
                pool.wait_ge(pool_own, k + 1)
                nc.gpsimd.tensor_tensor(var2[s][:, :], var[s][:, :], rstd[s][:, :], ALU.mult).then_inc(pool_own, 1)
                pool.wait_ge(pool_own, k + 2)
                nc.gpsimd.tensor_tensor(var2[s][:, :], var2[s][:, :], rstd[s][:, :], ALU.mult).then_inc(pool_own, 1)
                pool.wait_ge(pool_own, k + 3)
                nc.gpsimd.tensor_tensor(var2[s][:, :], var2[s][:, :], epsc[:, :], ALU.add).then_inc(pool_own, 1)
                pool.wait_ge(pool_own, k + 4)
                nc.gpsimd.tensor_tensor(r12[s][:, :], var2[s][:, :], mhalf[:, :], ALU.pow).then_inc(pool_own, 1)
                pool.wait_ge(pool_own, k + 5)
                nc.gpsimd.tensor_tensor(r12[s][:, :], r12[s][:, :], rstd[s][:, :], ALU.mult).then_inc(rs3, 1)

            two_by_two(pool, NG, rsqrt_twice)

            def slice_step(b, s):
                nc.gpsimd.tensor_copy(htb[s], cols(HT, b, SL)).then_inc(htb_ready, 1)

            pool.wait_ge(ht_ready, 1)
            pool.wait_ge(rows_clear, 16 * (NBLK * BS // 512))
            slice_step(0, 0)
            slice_step(1, 1)
            for k in range(2 * NE):
                whi, wlo = (w1h, w1l) if k < NE else (w2h, w2l)
                e, src = k % NE, wst[k % 2][:, :]
                pool.wait_ge(wst_in[k % 2], 16 * (k // 2 + 1))
                nc.gpsimd.tensor_copy(whi[:, e, :], src).then_inc(wsplit, 1)
                pool.wait_ge(wsplit, 2 * k + 1)
                nc.gpsimd.tensor_tensor(wlo[:, e, :], src, whi[:, e, :], ALU.subtract).then_inc(wsplit, 1)
            pool.wait_ge(ht_ready, NG)

            def next_slice(b, s):
                pool.wait_ge(v_done, b - 1)
                slice_step(b, s)

            with pool.Fori(1, SEQ0[1] // 2) as r:
                for s in range(2):
                    next_slice(2 * r + s, s)

            def norm5_step(i, s):
                rsqrt(i, s, norm5, rs5)
                nc.gpsimd.tensor_tensor(tiles(X, i), tiles(X, i), tiles(Z, i), ALU.add).then_inc(base_ready, 1)

            def scatter(n):
                for k in range(2):
                    pool.indirect_dma_start(xs, bass.IndirectOffsetOnAxis(idx[:, k, n:n + 1], 0),
                                            MH[:, n, :], None).then_inc(scattered[n // HN], 16)

            two_by_two(pool, GRP0[1], norm5_step)
            pool.wait_ge(lg_done, GRP0[1])
            next_slice(SEQ0[1], 0)
            next_slice(SEQ0[1] + 1, 1)
            pool.wait_ge(mh_ready, GRP0[1])
            pool.wait_ge(idx_ready, 1)
            for n in range(HN):
                scatter(n)
                b = SEQ0[1] + 2 + n // 4
                if n % 4 == 3 and b < NB:
                    next_slice(b, b % 2)
            two_by_two(pool, NG, norm5_step, lo=GRP0[1])
            pool.wait_ge(mh_ready, NG)
            pool.wait_ge(idx_ready, 2)
            for n in range(HN, NT):
                scatter(n)
            pool.wait_ge(base_ready, NG)
            pool.wait_ge(scattered[0], 32 * HN)
            pool.wait_ge(scattered[1], 32 * (NT - HN))
            for part in range(2):
                for s in range(2):
                    pool.wait_ge(yb_out[s], 8 * BLK0[part + 1])
                for n in range(TILE0[part], TILE0[part + 1]):
                    done = gat_in[1 + (n - HN) // 4 if part else 0]
                    for k in range(2):
                        pool.indirect_dma_start(gat[k][:, n, :], None, ys[0:BS * BLK0[part + 1], :],
                                                bass.IndirectOffsetOnAxis(idx[:, k, n:n + 1], 0))\
                            .then_inc(done, 16)

        @block.scalar
        def _(act):
            def copy(dst, src):
                return nc.scalar.activation(dst, src, ACT.Copy)

            def evac1(i, s):
                act.wait_ge(tp1, i + 1)
                copy(cols(HT, i, 512), bank[6 + s][:, :]).then_inc(xt_ready, 1)

            two_by_two(act, NG, evac1)
            act.wait_ge(bias_ready, 1)
            nc.scalar.activation(h0g[:, :], h0s[:, :], ACT.Sigmoid).then_inc(act_gates, 1)

            def gates(i, s):
                used(act, scan_done, 4 * (i - 1))
                for u in range(2):
                    act.wait_ge(hg_done, 2 * i + u + 1)
                    H_, G_ = bank[2 * u][0:HC, :], bank[2 * u + 1][0:HC, :]
                    nc.scalar.activation(zg[s][:, u, :], G_, ACT.Sigmoid, bias=bhg[:, 2 + u:3 + u])
                    nc.scalar.activation(ag[s][:, u, :], G_, ACT.Sigmoid, bias=nbg[:, u:u + 1], scale=-1.0)
                    nc.scalar.activation(sh[s][:, u, :], H_, ACT.Sigmoid, bias=bhg[:, u:u + 1])\
                        .then_inc(act_gates, 1)

            gates(0, 0)
            peeled(act, NG, gates)
            gates(NG - 1, 1)

            def evac3(i, s):
                act.wait_ge(nmr_ready, i + 1)
                for t in range(4):
                    last = nc.scalar.activation(tile(Z, 4 * i + t), tile(X, 4 * i + t), ACT.Identity,
                                                bias=nmr[s][:, t:t + 1], scale=rstd[s][:, t:t + 1])
                last.then_inc(z_ready, 1)
                act.wait_ge(tp3, i + 1)
                nc.scalar.activation(cols(HT, i, 512), bank[6 + s][:, :], ACT.Identity,
                                     bias=aff[:, 1:2], scale=aff[:, 0:1]).then_inc(ht_ready, 1)

            two_by_two(act, NG, evac3)

            def front_hi(n, s):
                act.wait_ge(qk_done, n + 1)
                copy(hi[s], bank[7][:, :]).then_inc(hi_ready, 1)

            def front_ka(n):
                used(act, km_ready, n)
                for half in range(2):
                    act.wait_ge(selk_done, 2 * n + half + 1)
                    nc.scalar.activation(flat(KA[:, 2 * half:2 * half + 2, :]), bank[6 + half][:, :],
                                         ACT.Identity, bias=mask[4]).then_inc(ka_ready, 1)

            def front_qa(n, s):
                for half in range(2):
                    act.wait_ge(selq_done, 2 * n + half + 1)
                    copy(flat(QA[s][:, 2 * half:2 * half + 2, :]), bank[6 + half][:, :]).then_inc(qa_ready, 1)

            def front_qm(n, s, half):
                act.wait_ge(selm_done, 2 * n + half + 1)
                copy(flat(QM[s][:, 2 * half:2 * half + 2, :]), bank[7 - half][:, :]).then_inc(qm_ready, 1)

            def exp_step(b, c):
                act.wait_ge(st_done, 16 * b + c + 1)
                used(act, pv_done, 16 * b + c - 3)
                nc.scalar.activation(PT[c % 4], bank[2 + c % 2][:, :], ACT.Exp, scale=DH ** -0.5)\
                    .then_inc(exp_done, 1)

            def ctx_evac(b, pair):
                act.wait_ge(pv_done, 16 * b + 8 * pair + 8)
                used(act, ctt_done, 2 * b)
                copy(flat(CT[:, 2 * pair:2 * pair + 2, :]), bank[4 + pair][:, :]).then_inc(ct_ready, 1)

            def attention(b, s, front=True, nxt=True, tail=True):
                for c in range(16):
                    exp_step(b, c)
                    if tail and c == 0:
                        ctx_evac(b - 1, 1)
                    if tail and c == 1:
                        front_qm(b, s, 1)
                    if front and c == 6:
                        front_hi(b + 2, s)
                    if front and c == 8:
                        front_ka(b + 2)
                    if front and c == 9:
                        front_qa(b + 2, s)
                    if c == 10:
                        ctx_evac(b, 0)
                    if nxt and c == 12:
                        front_qm(b + 1, 1 - s, 0)

            def evac5(i, s):
                act.wait_ge(xh5, i + 1)
                copy(tiles(MH, i), xh[s][:, :, :]).then_inc(mh_ready, 1)
                act.wait_ge(tp5, i + 1)
                used(act, lg_done, i - 1)
                nc.scalar.activation(MT[s], bank[6 + s][:, :], ACT.Identity,
                                     bias=aff[:, 3:4], scale=aff[:, 2:3]).then_inc(mt_ready, 1)

            for part in range(2):
                first = SEQ0[part]
                if part:
                    act.wait_ge(route_done, 1)
                for s in range(2):
                    front_hi(first + s, s)
                    front_ka(first + s)
                    front_qa(first + s, s)
                    if s == 0:
                        for h in range(2):
                            front_qm(first, 0, h)
                sequences(act, first, attention)
                ctx_evac(SEQ0[part + 1] - 1, 1)
                two_by_two(act, GRP0[part + 1], evac5, lo=GRP0[part])
                act.wait_ge(dif_ready, part + 1)
                n = TILE0[part + 1] - TILE0[part]
                nc.scalar.activation(w_2[:, 0:n], dif[:, 0:n], ACT.Exp).then_inc(exp6, 1)

            act.wait_ge(tab_ready, 2)

            def load_block(b, q):
                act.dma_start(XB[q], xs[bass.ds(b * BS, BS), :].rearrange("(h p) d -> p h d", p=P))\
                  .then_inc(xb_in[q], 16)

            def x_hi(b, q):
                s = q % 2
                act.wait_ge(tp7, b + 1)
                if exists(b + 4):
                    load_block(b + 4, q)
                used(act, up_done, b - 1)
                nc.scalar.activation(xmh[s], bank[s][:, 0:BS], ACT.Identity,
                                     bias=aff[:, 3:4], scale=aff[:, 2:3]).then_inc(xmh_ready, 1)

            def gelu(b, s):
                e = act.value_load(blke[0:1, bass.ds(b, 1)], min_val=0, max_val=NE - 1)
                act.wait_ge(up_done, b + 1)
                used(act, gl_ready, b - 1)
                for c in range(FC):
                    last = nc.scalar.activation(G32[s][:, BS * c:BS * c + BS],
                                                bank[2 + 2 * s + c // 2][:, BS * (c % 2):BS * (c % 2) + BS],
                                                ACT.Gelu_apprx_tanh, bias=b1s[:, bass.ds(e * FC + c, 1)])
                last.then_inc(gelu_done, 1)

            def experts(b, q):
                if exists(b + 3):
                    x_hi(b + 3, (q + 3) % 4)
                if exists(b + 2):
                    gelu(b + 2, q % 2)

            act.wait_ge(scattered[0], 32 * HN)
            for q in range(4):
                load_block(q, q)
            blocks(act, -3, experts, second_part=lambda: act.wait_ge(scattered[1], 32 * (NT - HN)))

        @block.vector
        def _(dve):
            V = nc.vector
            count = [0]

            for s in range(2):
                V.memset(ot[s][HC:HC + 1, :, :], 1.0).then_inc(row_ones, 1)

            def moments(i, s, buf, base, done):
                k = base + 3 * i
                for t in range(4):
                    last = V.bn_stats(mom[:, t, :], tile(buf, 4 * i + t))
                last.then_inc(dve_own, 1)
                dve.wait_ge(dve_own, k + 1)
                V.tensor_tensor(ssum[:, :], mom[:, :, 1], mom[:, :, 4], ALU.add)
                V.tensor_tensor(sdif[:, :], mom[:, :, 1], mom[:, :, 4], ALU.subtract)
                V.tensor_tensor(sm2[:, :], mom[:, :, 2], mom[:, :, 5], ALU.add).then_inc(dve_own, 1)
                dve.wait_ge(dve_own, k + 2)
                V.tensor_scalar(mean[s][:, :], ssum[:, :], 0.5, None, ALU.mult)
                V.scalar_tensor_tensor(sq[:, :], sdif[:, :], 0.25, sdif[:, :], ALU.mult, ALU.mult)
                V.tensor_scalar(sm2[:, :], sm2[:, :], 1.0 / D, None, ALU.mult).then_inc(dve_own, 1)
                dve.wait_ge(dve_own, k + 3)
                V.tensor_tensor(var[s][:, :], sm2[:, :], sq[:, :], ALU.add)
                V.scalar_tensor_tensor(vare[s][:, :], sm2[:, :], EPS, sq[:, :], ALU.add, ALU.add).then_inc(done, 1)

            def normed(i, s, buf, rs, done, dst=None, src=None):
                for t in range(4):
                    last = V.tensor_scalar(xh[s][:, t, :] if dst is None else tile(dst, 4 * i + t),
                                           tile(buf, 4 * i + t), mean[s][:, t:t + 1],
                                           (src or rstd)[s][:, t:t + 1], ALU.subtract, ALU.mult)
                if done is not None:
                    last.then_inc(done, 1)

            def moments1(i, s):
                dve.wait_ge(x_in[s], 8 * (i - s) + 16)
                moments(i, s, X, 0, norm1)

            def normed1(i, s):
                dve.wait_ge(rs1, i + 1)
                used(dve, tp1, i - 1)
                normed(i, s, X, rs1, xh1)

            skewed(dve, NG, moments1, normed1)
            dve.wait_ge(const_in, 16)
            dve.wait_ge(params_in, 16 * NPAR)
            V.tensor_scalar(nbg[:, :], bhg[:, 2:4], -1.0, None, ALU.mult)
            V.tensor_scalar(h0t[:, :], h0s[:, :], 0.0, None, ALU.max).then_inc(bias_ready, 1)
            own1 = 3 * NG
            dve.wait_ge(act_gates, 1)
            V.scalar_tensor_tensor(h0g[:, :], h0g[:, :], 0.5, h0t[:, :], ALU.min, ALU.add).then_inc(dve_own, 1)
            dve.wait_ge(dve_own, own1 + 1)

            def gates(i, s):
                for u in range(2):
                    dve.wait_ge(act_gates, 2 * i + u + 2)
                    V.tensor_scalar(hv[s][:, u, :], bank[2 * u][0:HC, :], bhg[:, u:u + 1], 0.0,
                                    ALU.add, ALU.max).then_inc(relu_done, 1)
                    dve.wait_ge(relu_done, 2 * i + u + 1)
                    V.scalar_tensor_tensor(hv[s][:, u, :], sh[s][:, u, :], 0.5, hv[s][:, u, :],
                                           ALU.min, ALU.add).then_inc(g_ready, 1)

            def scans(i, s):
                for u in range(2):
                    dve.wait_ge(v_ready, 2 * i + u + 1)
                    for b in range(2):
                        t = slice(SL * b, SL * b + SL)
                        V.tensor_tensor_scan(ot[s][0:HC, u, t], ag[s][:, u, t], zg[s][:, u, t],
                                             h0g[:, u:u + 1], ALU.mult, ALU.add).then_inc(scan_done, 1)

            def add_y(i, s):
                dve.wait_ge(y_done, i + 1)
                V.tensor_tensor(tiles(X, i), bank[4 + s][:, :].rearrange("p (n d) -> p n d", d=D),
                                tiles(X, i), ALU.add).then_inc(x1_ready, 1)

            def recurrence(i, s):
                gates(i, s)
                add_y(i - 1, 1 - s)
                scans(i, s)

            gates(0, 0)
            scans(0, 0)
            peeled(dve, NG, recurrence)
            recurrence(NG - 1, 1)
            add_y(NG - 1, 1)

            def moments3(i, s):
                dve.wait_ge(x1_ready, i + 1)
                moments(i, s, X, own1 + 1, norm3)

            def normed3(i, s):
                dve.wait_ge(rs3, i + 1)
                used(dve, tp3, i - 1)
                used(dve, z_ready, i - 1)
                V.scalar_tensor_tensor(nmr[s][:, :], mean[s][:, :], -1.0, rstd[s][:, :],
                                       ALU.mult, ALU.mult).then_inc(nmr_ready, 1)
                normed(i, s, X, rs3, xh3, src=r12)

            skewed(dve, NG, moments3, normed3)
            own3 = own1 + 1 + 3 * NG

            def front_lo(n, s):
                dve.wait_ge(hi_ready, n + 1)
                V.scalar_tensor_tensor(lo[s], hi[s], -1.0, bank[7][:, :], ALU.mult, ALU.add)\
                    .then_inc(lo_ready, 1)

            def front_v(n, s):
                dve.wait_ge(v_done, n + 1)
                used(dve, pv_done, 16 * (n - 1))
                V.tensor_copy(VA[s][:, :, :, 0:DH],
                              bank[6][:, 0:2 * D].rearrange("p (k h d) -> p k h d", k=2, d=DH))\
                    .then_inc(va_ready, 1)

            def front_mask(n, s):
                dve.wait_ge(ka_ready, 2 * n + 2)
                used(dve, st_done, 16 * (n - 1))
                for j in range(4):
                    last = V.tensor_scalar(KM[s][:, :, j, :], KA, mask[j], None, ALU.mult)
                last.then_inc(km_ready, 1)

            def max_chunk(n, c):
                g, qt, jp = c // 4, c // 2 % 2, c % 2
                dve.wait_ge(s_done, 16 * n + c + 1)
                V.tensor_reduce(nmax[:, qt, 4 * g + 2 * jp:4 * g + 2 * jp + 2],
                                bank[c % 2][:, :].rearrange("p (j t) -> p j t", j=2),
                                AX.X, ALU.max, negate=True).then_inc(max_done, 1)
                if c in (11, 15):
                    half, k = c // 15, H // 2 * (1 + c // 15)
                    dve.wait_ge(nmt_done, 2 * n + half + 1)
                    V.tensor_scalar(nmt[half][0:k, :], bank[6][0:k, 0:SL], 1.0 / MUL, None, ALU.mult)\
                        .then_inc(nmt_ready, 1)

            def tail_norm(m):
                for qt in range(2):
                    dve.wait_ge(ctt_done, 2 * m + qt + 1)
                    src = bank[6 + qt][:, :].rearrange("p (h r) -> p h r", r=32)
                    V.reciprocal(rden[:, qt, :], src[:, :, DH]).then_inc(den_ready, 1)
                    dve.wait_ge(den_ready, 2 * m + qt + 1)
                    V.tensor_tensor(CN[:, qt, :].rearrange("p (h d) -> p h d", d=DH), src[:, :, 0:DH],
                                    rden[:, qt, :, None].broadcast_to([P, H, DH]), ALU.mult)\
                        .then_inc(cn_ready, 1)

            def tail_copy(m):
                dve.wait_ge(cnt_done, m + 1)
                V.tensor_copy(CNT, bank[6][:, 0:SL]).then_inc(cnt_ready, 1)

            def tail_out(m):
                dve.wait_ge(wo_done, m + 1)
                z2 = Z[:, bass.ds(2 * m, 2), :]
                V.tensor_tensor(z2, bank[7][:, 0:2 * D].rearrange("p (n d) -> p n d", d=D), z2, ALU.add)\
                    .then_inc(x3_ready, 1)

            def attention(b, s, front=True, nxt=True, tail=True):
                n = b + 1
                if nxt:
                    front_mask(n, 1 - s)
                    max_chunk(n, 0)
                    max_chunk(n, 1)
                if tail:
                    tail_norm(b - 1)
                for c in range(2, 16):
                    if nxt:
                        max_chunk(n, c)
                    if tail and c == 3:
                        tail_copy(b - 1)
                    if tail and c == 4:
                        tail_out(b - 1)
                    if nxt and c == 4:
                        front_v(n, 1 - s)
                    if front and c == 6:
                        front_lo(b + 2, s)

            dve.wait_ge(preset, 4)
            dve.wait_ge(ht_ready, NG)

            def moments5(i, s):
                dve.wait_ge(x3_ready, 2 * i + 2)
                moments(i, s, Z, base5, norm5)

            def normed5(i, s):
                dve.wait_ge(rs5, i + 1)
                used(dve, tp5, i - 1)
                used(dve, mh_ready, i - 1)
                normed(i, s, Z, rs5, xh5)

            k = [own3]

            def step(ins):
                ins.then_inc(dve_own, 1)
                k[0] += 1
                dve.wait_ge(dve_own, k[0])

            def by_tile(v):
                return v.rearrange("p (n e) -> p n e", e=NE)

            def by_expert(v):
                return v.rearrange("p (e n) -> p e n", e=NE)

            def route(part):
                nt, nb = TILE0[part + 1] - TILE0[part], BLK0[part + 1] - BLK0[part]
                lg, key, oh1, oh2, l2, ohs, cum, dst, prd = (v[:, 0:nt * NE] for v in by_pair)
                m1, m2, r1, r2, w_1, w_2, dif, d1f, d2f = (v[:, 0:nt] for v in by_token)
                of_tiles = slice(TILE0[part], TILE0[part + 1])
                of_blocks = slice(BLK0[part], BLK0[part + 1])

                def over_e(v):
                    return v[:, :, None].broadcast_to([P, nt, NE])

                keys = cst[:, None, C_KEY:C_KEY + NE].broadcast_to([P, nt, NE])
                dve.wait_ge(lg_done, GRP0[part + 1])
                dve.wait_ge(ones_ready, 1)
                step(V.tensor_copy(lg, bank[0][:, NE * TILE0[part]:NE * TILE0[part + 1]]))
                for src, oh, m, r in ((lg, oh1, m1, r1), (l2, oh2, m2, r2)):
                    step(V.tensor_reduce(m, by_tile(src), AX.X, ALU.max))
                    step(V.tensor_tensor(by_tile(key), by_tile(src), over_e(m), ALU.is_equal))
                    step(V.tensor_tensor(by_tile(key), by_tile(key), keys, ALU.mult))
                    step(V.tensor_reduce(r, by_tile(key), AX.X, ALU.max))
                    step(V.tensor_tensor(by_tile(oh), by_tile(key), over_e(r), ALU.is_equal))
                    if src is lg:
                        step(V.scalar_tensor_tensor(l2, oh1, -BIG, lg, ALU.mult, ALU.add))
                V.tensor_tensor(dif, m2, m1, ALU.subtract).then_inc(dif_ready, 1)
                step(V.tensor_tensor(by_expert(ohs).rearrange("p e n -> p n e"), by_tile(oh1), by_tile(oh2), ALU.add))
                V.tensor_reduce(tot, by_expert(ohs), AX.X, ALU.add).then_inc(tot_ready, 1)
                step(V.tensor_tensor_scan(cum, ones[:, 0:1].broadcast_to([P, NE * nt]), ohs, 0.0, ALU.mult, ALU.add))
                step(V.tensor_tensor(cum, cum, ohs, ALU.subtract))
                dve.wait_ge(cnt_sum, part + 1)
                step(V.tensor_scalar(cntn[:, :], bank[1][:, 0:NE], float(BS - 1), None, ALU.add))
                step(V.tensor_scalar(cntn[:, :], cntn[:, :], BS.bit_length() - 1, None, ALU.logical_shift_right))
                step(V.tensor_copy(nblk, cntn[:, :]))
                step(V.tensor_tensor_scan(endb, ones[:, 0:NE], nblk, float(BLK0[part]), ALU.mult, ALU.add))
                step(V.tensor_tensor(off, endb, nblk, ALU.subtract))
                step(V.scalar_tensor_tensor(off, off, float(BS), bank[2][:, 0:NE], ALU.mult, ALU.add))
                step(V.tensor_tensor(off, off, by_expert(cum)[:, :, 0], ALU.subtract))
                step(V.tensor_tensor(by_expert(dst), by_expert(cum), off[:, :, None].broadcast_to([P, NE, nt]), ALU.add))
                for q, (oh, df) in enumerate(((oh1, d1f), (oh2, d2f))):
                    step(V.tensor_tensor(by_tile(prd), by_tile(oh), by_expert(dst).rearrange("p e n -> p n e"), ALU.mult))
                    step(V.tensor_reduce(df, by_tile(prd), AX.X, ALU.add))
                    last = V.tensor_copy(idx[:, q, of_tiles], df)
                last.then_inc(idx_ready, 1)
                step(V.tensor_tensor(blkc[:, 0:nb, :], blkn[:, of_blocks, None].broadcast_to([1, nb, NE]),
                                     endb[0:1, None, :].broadcast_to([1, nb, NE]), ALU.is_ge))
                step(V.tensor_reduce(blkf[:, 0:nb], blkc[:, 0:nb, :], AX.X, ALU.add))
                V.tensor_scalar(blke[:, of_blocks], blkf[:, 0:nb], float(NE - 1), None, ALU.min).then_inc(tab_ready, 1)
                dve.wait_ge(exp6, part + 1)
                step(V.tensor_scalar(w_1, w_2, 1.0, None, ALU.add))
                step(V.reciprocal(wts[:, 0, of_tiles], w_1))
                V.tensor_tensor(wts[:, 1, of_tiles], w_2, wts[:, 0, of_tiles], ALU.mult).then_inc(route_done, 1)
                for done in (idx_ready, tab_ready, route_done):
                    dve.wait_ge(done, part + 1)

            for part in range(2):
                first, last = SEQ0[part], SEQ0[part + 1] - 1
                for h in range(2):
                    V.memset(nmt[h], 0.0)
                front_lo(first, 0)
                front_v(first, 0)
                front_mask(first, 0)
                for c in range(16):
                    max_chunk(first, c)
                front_lo(first + 1, 1)
                sequences(dve, first, attention)
                tail_norm(last)
                tail_copy(last)
                tail_out(last)
                base5 = k[0] - 3 * GRP0[part]
                skewed(dve, GRP0[part + 1], moments5, normed5, lo=GRP0[part])
                k[0] += 3 * (GRP0[part + 1] - GRP0[part])
                route(part)


            def x_lo(b, s):
                dve.wait_ge(xmh_ready, b + 1)
                used(dve, xml_ready, b)
                V.tensor_scalar(xm, bank[s][:, 0:BS], aff[:, 2:3], aff[:, 3:4], ALU.mult, ALU.add)\
                    .then_inc(xm_own, 1)
                dve.wait_ge(xm_own, b + 1)
                V.tensor_tensor(xml[s], xm, xmh[s], ALU.subtract).then_inc(xml_ready, 1)

            def split(b, s):
                dve.wait_ge(gelu_done, b + 1)
                used(dve, down_done, b - 1)
                V.tensor_copy(GH[s], G32[s]).then_inc(gh_own, 1)
                dve.wait_ge(gh_own, b + 1)
                V.tensor_tensor(GL[s], G32[s], GH[s], ALU.subtract).then_inc(gl_ready, 1)

            def y_out(b, s):
                e = dve.value_load(blke[0:1, bass.ds(b, 1)], min_val=0, max_val=NE - 1)
                dve.wait_ge(down_done, b + 1)
                used(dve, yb_out[s], 8 * (b - s))
                V.tensor_tensor(YB[s], bank[6 + s][:, 0:2 * D].rearrange("p (h d) -> p h d", d=D),
                                b2s[:, bass.ds(e, 1), :].broadcast_to([P, 2, D]), ALU.add).then_inc(yb_ready, 1)

            def experts(b, q):
                if exists(b + 3):
                    x_lo(b + 3, (q + 1) % 2)
                if exists(b + 1):
                    split(b + 1, (q + 1) % 2)
                if exists(b - 1):
                    y_out(b - 1, (q + 1) % 2)

            blocks(dve, -3, experts)
            y_out(NBLK - 1, 1)

            dve.wait_ge(base_ready, NG)
            for i in range(NG):
                if i < GRP0[1]:
                    dve.wait_ge(gat_in[0], 32 * HN)
                else:
                    dve.wait_ge(gat_in[1 + i - GRP0[1]], 32 * 4)
                used(dve, comb, i)
                for t in range(4):
                    n = 4 * i + t
                    last = V.scalar_tensor_tensor(cmb[:, t, :], gat[0][:, n, :], wts[:, 0, n:n + 1],
                                                  X[:, n, :], ALU.mult, ALU.add)
                last.then_inc(cmb_own, 1)
                if i >= 2:
                    dve.wait_ge(o_out[i % 2], 16 * (i // 2))
                dve.wait_ge(cmb_own, i + 1)
                for t in range(4):
                    n = 4 * i + t
                    last = V.scalar_tensor_tensor(ob[i % 2][:, t, :], gat[1][:, n, :], wts[:, 1, n:n + 1],
                                                  cmb[:, t, :], ALU.mult, ALU.add)
                last.then_inc(comb, 1)

        @block.tensor
        def _(pe):
            def mm(dst, lhsT, rhs, start=True, stop=True):
                return nc.tensor.matmul(dst, lhsT, rhs, start=start, stop=stop)

            def transposes(bk, src, done):
                for t in range(4):
                    last = nc.tensor.transpose(bk[:, P * t:P * t + P], src[:, t, :], ident)
                last.then_inc(done, 1)

            pe.wait_ge(const_in, 16)

            def tp1_step(i, s):
                pe.wait_ge(xh1, i + 1)
                used(pe, xt_ready, i - 1)
                transposes(bank[6 + s], xh[s], tp1)

            two_by_two(pe, NG, tp1_step)

            pe.wait_ge(params_in, 16 * NPAR)
            pe.wait_ge(row_ones, 2)

            def hidden_gate(i, s):
                pe.wait_ge(xt_ready, i + 1)
                for u in range(2):
                    used(pe, act_gates, 2 * i + u)
                    used(pe, relu_done, 2 * i + u - 1)
                    mm(bank[2 * u][0:HC, :], whg[:, u, :], cols(HT, i, 512))
                    mm(bank[2 * u + 1][0:HC, :], whg[:, 2 + u, :], cols(HT, i, 512)).then_inc(hg_done, 1)

            def y_step(i, s):
                pe.wait_ge(scan_done, 4 * i + 4)
                used(pe, x1_ready, i - 1)
                for t in range(4):
                    for u in range(2):
                        k = HC + u
                        last = mm(bank[4 + s][:, P * t:P * t + P], ot[s][0:k, u, P * t:P * t + P],
                                  wout[0:k, u, :], start=u == 0, stop=u == 1)
                last.then_inc(y_done, 1)

            skewed(pe, NG, hidden_gate, y_step)

            def tp3_step(i, s):
                pe.wait_ge(xh3, i + 1)
                used(pe, ht_ready, i - 1)
                transposes(bank[6 + s], xh[s], tp3)

            two_by_two(pe, NG, tp3_step)

            def banks_free(n):
                if n == 0:
                    pe.wait_ge(ht_ready, NG)
                elif n == SEQ0[1]:
                    pe.wait_ge(route_done, 1)
                else:
                    pe.wait_ge(qm_ready, 2 * n)

            def proj_qk(n, s, tail=False):
                pe.wait_ge(htb_ready, n + 1)
                if tail:
                    pe.wait_ge(x3_ready, n - 2)
                mm(bank[7][:, 0:SL], wqk[:, 0, :], htb[s])
                mm(bank[7][:, SL:2 * SL], wqk[:, 1, :], htb[s]).then_inc(qk_done, 1)

            def proj_v(n, s, tail=False, second=False):
                if tail:
                    pe.wait_ge(cnt_ready, n - 1)
                elif second:
                    pe.wait_ge(qa_ready, 2 * n + 2)
                for kt in range(2):
                    last = mm(bank[6][:, P * kt:P * kt + P], htb[s][:, P * kt:P * kt + P], wvo[:, 0, :])
                last.then_inc(v_done, 1)

            def rows(n, parts, bk, half, done):
                for gi in range(2):
                    g = 2 * half + gi
                    for k, (sl, src) in enumerate(parts):
                        last = mm(bk[:, SL * gi:SL * gi + SL], sel[:, sl, g, :], src,
                                  start=k == 0, stop=k == len(parts) - 1)
                last.then_inc(done, 1)

            q_, k_ = slice(0, SL), slice(SL, 2 * SL)

            def sel_k(n, s):
                pe.wait_ge(lo_ready, n + 1)
                used(pe, va_ready, n)
                for half in range(2):
                    rows(n, ((0, hi[s][:, k_]), (1, lo[s][:, k_])), bank[6 + half], half, selk_done)

            def sel_q(n, s):
                for half in range(2):
                    pe.wait_ge(ka_ready, 2 * n + half + 1)
                    rows(n, ((2, hi[s][:, q_]), (3, lo[s][:, q_])), bank[6 + half], half, selq_done)

            def s_chunk(n, s, c):
                g, qt, jp = c // 4, c // 2 % 2, c % 2
                if c == 0:
                    pe.wait_ge(km_ready, n + 1)
                if c % 8 == 0:
                    pe.wait_ge(qa_ready, 2 * n + c // 8 + 1)
                used(pe, max_done, 16 * n + c - 1)
                mm(bank[c % 2][:, :], QA[s][:, g, P * qt:P * qt + P],
                   KM[s][:, g, 2 * jp:2 * jp + 2, :]).then_inc(s_done, 1)

            def max_rows(n, half, front):
                pe.wait_ge(max_done, 16 * n + 8 * half + 8)
                if half == 0 and front:
                    pe.wait_ge(qa_ready, 2 * n + 3)
                k = H // 2 * (1 + half)
                for qt in range(2):
                    last = mm(bank[6][0:k, P * qt:P * qt + P], nmax[:, qt, 0:k], ident)
                last.then_inc(nmt_done, 1)

            def sel_m(n, s, half, front, tail=False):
                pe.wait_ge(nmt_ready, 2 * n + half + 1)
                if half == 0 and front:
                    pe.wait_ge(qa_ready, 2 * n + 4)
                elif half == 0 and tail:
                    pe.wait_ge(x3_ready, n - 1)
                rows(n, ((2, hi[s][:, q_]), (3, lo[s][:, q_]), (4, nmt[half])), bank[7 - half], half, selm_done)

            def st_chunk(b, s, c):
                g, kt, jp = c // 4, c // 2 % 2, c % 2
                if c % 8 == 0:
                    pe.wait_ge(qm_ready, 2 * b + c // 8 + 1)
                used(pe, exp_done, 16 * b + c - 1)
                for jj in range(2):
                    last = mm(bank[2 + c % 2][:, SL * jj:SL * jj + SL],
                              KM[s][:, g, 2 * jp + jj, P * kt:P * kt + P], QM[s][:, g, :])
                last.then_inc(st_done, 1)

            def pv(b, s, c):
                g, kt, jp = c // 4, c // 2 % 2, c % 2
                pe.wait_ge(exp_done, 16 * b + c + 1)
                if c == 0:
                    pe.wait_ge(va_ready, b + 1)
                if c % 8 == 0:
                    used(pe, ct_ready, 2 * b - 1 + c // 8)
                for jj in range(2):
                    j = 2 * jp + jj
                    last = mm(bank[4 + g // 2][32 * j:32 * j + 32, SL * (g % 2):SL * (g % 2) + SL],
                              VA[s][:, kt, 4 * g + j, :], PT[c % 4][:, SL * jj:SL * jj + SL],
                              start=kt == 0, stop=kt == 1)
                last.then_inc(pv_done, 1)

            def ctx_t(m, last=False):
                pe.wait_ge(ct_ready, 2 * m + 2)
                if last:
                    pe.wait_ge(x3_ready, m)
                else:
                    pe.wait_ge(qm_ready, 2 * m + 4)
                for qt in range(2):
                    for g in range(4):
                        last = nc.tensor.transpose(bank[6 + qt][:, P * g:P * g + P],
                                                   CT[:, g, P * qt:P * qt + P], ident)
                    last.then_inc(ctt_done, 1)

            def ctx_n(m):
                pe.wait_ge(cn_ready, 2 * m + 2)
                for qt in range(2):
                    last = nc.tensor.transpose(bank[6][:, P * qt:P * qt + P], CN[:, qt, :], ident)
                last.then_inc(cnt_done, 1)

            def ctx_o(m):
                pe.wait_ge(cnt_ready, m + 1)
                for qt in range(2):
                    last = mm(bank[7][:, P * qt:P * qt + P], CNT[:, P * qt:P * qt + P], wvo[:, 1, :])
                last.then_inc(wo_done, 1)

            def attention(b, s, front=True, nxt=True, tail=True):
                n, ns, f = b + 1, 1 - s, b + 2
                after_st = {2: 0, 3: 2, 4: 3, 5: 4, 6: 6, 7: 7, 8: 8, 9: 10, 10: 11, 11: 12, 12: 14, 13: 15}
                after_pv = {5: 5, 8: 9, 11: 13}
                st_chunk(b, s, 0)
                st_chunk(b, s, 1)
                for c in range(2, 16):
                    st_chunk(b, s, c)
                    if nxt and c in after_st:
                        s_chunk(n, ns, after_st[c])
                    pv(b, s, c - 2)
                    if nxt and c == 2:
                        s_chunk(n, ns, 1)
                    if tail and c == 2:
                        ctx_t(b - 1)
                    if tail and c == 4:
                        ctx_n(b - 1)
                    if tail and c == 5:
                        ctx_o(b - 1)
                    if nxt and c == 5:
                        proj_v(n, ns, tail, second=not tail)
                    if front and c == 6:
                        proj_qk(f, s, tail)
                    if front and c == 8:
                        sel_k(f, s)
                    if front and c == 9:
                        sel_q(f, s)
                    if nxt and c == 10:
                        max_rows(n, 0, front)
                    if nxt and c == 11:
                        sel_m(n, ns, 0, front, tail)
                    if nxt and c == 14:
                        max_rows(n, 1, front)
                    if nxt and c in after_pv:
                        s_chunk(n, ns, after_pv[c])
                pv(b, s, 14)
                if nxt:
                    sel_m(n, ns, 1, front)
                pv(b, s, 15)

            def tp5_step(i, s):
                pe.wait_ge(xh5, i + 1)
                used(pe, mt_ready, i - 1)
                transposes(bank[6 + s], xh[s], tp5)

            def logits(i, s):
                pe.wait_ge(mt_ready, i + 1)
                for t in range(4):
                    last = mm(cols(bank[0], 4 * i + t, NE), MT[s][:, P * t:P * t + P], wgs[:, :])
                last.then_inc(lg_done, 1)

            for part in range(2):
                first, last = SEQ0[part], SEQ0[part + 1] - 1
                banks_free(first)
                proj_qk(first, 0)
                proj_v(first, 0)
                pe.wait_ge(va_ready, first + 1)
                sel_k(first, 0)
                sel_q(first, 0)
                for c in range(16):
                    s_chunk(first, 0, c)
                    if c == 11:
                        max_rows(first, 0, False)
                sel_m(first, 0, 0, False)
                max_rows(first, 1, False)
                sel_m(first, 0, 1, False)
                banks_free(first + 1)
                proj_qk(first + 1, 1)
                sel_k(first + 1, 1)
                sel_q(first + 1, 1)
                sequences(pe, first, attention)
                ctx_t(last, last=True)
                ctx_n(last)
                ctx_o(last)
                pe.wait_ge(x3_ready, last + 1)
                skewed(pe, GRP0[part + 1], tp5_step, logits, lo=GRP0[part])
                pe.wait_ge(tot_ready, part + 1)
                mm(bank[1][:, 0:NE], ones[:, 0:P], tot)
                mm(bank[2][:, 0:NE], cst[:, C_TRI:C_TRI + P], tot).then_inc(cnt_sum, 1)

            pe.wait_ge(tab_ready, 2)
            pe.wait_ge(wsplit, 4 * NE)

            def block_t(b, q):
                pe.wait_ge(xb_in[q], 4 * (b - q) + 16)
                used(pe, xml_ready, b - 1)
                for h in range(2):
                    last = nc.tensor.transpose(bank[q % 2][:, P * h:P * h + P], XB[q][:, h, :], ident)
                last.then_inc(tp7, 1)

            def expert_of(b):
                return pe.value_load(blke[0:1, bass.ds(b, 1)], min_val=0, max_val=NE - 1)

            def part(w, e, c):
                return w[:, bass.ds(e, 1), P * c:P * c + P].rearrange("p a f -> p (a f)")

            def up(b, s):
                e = expert_of(b)
                pe.wait_ge(xml_ready, b + 1)
                used(pe, gelu_done, b - 1)
                for c in range(FC):
                    dst = bank[2 + 2 * s + c // 2][:, BS * (c % 2):BS * (c % 2) + BS]
                    mm(dst, part(w1h, e, c), xmh[s], stop=False)
                    mm(dst, part(w1h, e, c), xml[s], start=False, stop=False)
                    last = mm(dst, part(w1l, e, c), xmh[s], start=False)
                last.then_inc(up_done, 1)

            def down(b, s):
                e = expert_of(b)
                pe.wait_ge(gl_ready, b + 1)
                used(pe, yb_ready, b - 1)
                for h in range(2):
                    dst = bank[6 + s][:, P * h:P * h + P]
                    for c in range(FC):
                        x = slice(BS * c + P * h, BS * c + P * h + P)
                        mm(dst, GH[s][:, x], part(w2h, e, c), start=c == 0, stop=False)
                        mm(dst, GH[s][:, x], part(w2l, e, c), start=False, stop=False)
                        last = mm(dst, GL[s][:, x], part(w2h, e, c), start=False, stop=c == FC - 1)
                last.then_inc(down_done, 1)

            def experts(b, q):
                if exists(b + 3):
                    block_t(b + 3, (q + 3) % 4)
                if exists(b + 2):
                    up(b + 2, q % 2)
                if exists(b):
                    down(b, q % 2)

            blocks(pe, -3, experts)


def kernel(**inputs):
    import concourse.bacc as bacc
    from concourse.bass_utils import run_bass_kernel_spmd

    a = {k: np.asarray(v) for k, v in inputs.items()}
    const, const_sel, const_blk = constants()
    arrays = {
        "x": a["L0_attn_x"],
        "w_hg": a["L0_attn_W_hg"].T,
        "b_hg": a["L0_attn_b_hg"].reshape(4, HC).T,
        "w_out": a["L0_attn_W_out"].T,
        "b_out": a["L0_attn_b_out"].reshape(1, D),
        "h0": a["L0_attn_h0"].reshape(2, HC).T,
        "g1": a["L0_ffn_ln1_g"].reshape(D, 1),
        "be1": a["L0_ffn_ln1_b"].reshape(D, 1),
        "g2": a["L0_ffn_ln2_g"].reshape(D, 1),
        "be2": a["L0_ffn_ln2_b"].reshape(D, 1),
        "wq": a["L0_ffn_Wq"],
        "wk": a["L0_ffn_Wk"],
        "wv": a["L0_ffn_Wv"],
        "wo": a["L0_ffn_Wo"],
        "wg": a["L0_ffn_Wg"],
        "w1": a["L0_ffn_W1"],
        "b1": a["L0_ffn_b1"].reshape(NE, FC, P).transpose(2, 0, 1).reshape(P, NE * FC),
        "w2": a["L0_ffn_W2"],
        "b2": a["L0_ffn_b2"],
        "const": const,
        "const_sel": const_sel,
        "const_blk": const_blk,
    }
    arrays = {k: np.ascontiguousarray(v) for k, v in arrays.items()}
    nc = bacc.Bacc("TRN2", target_bir_lowering=False, num_devices=1)
    args = [nc.dram_tensor(k, v.shape, mybir.dt.from_np(v.dtype), kind="ExternalInput").ap()
            for k, v in arrays.items()]
    args.append(nc.dram_tensor("out", (NB, SL, D), F32, kind="ExternalOutput").ap())
    layer_kernel(nc, *args)
    return run_bass_kernel_spmd(nc, [arrays], core_ids=[0]).results[0]["out"]
```
